# Optimizing a Trainium2 kernel written in Bass

```python
import numpy as np
import jax
import jax.numpy as jnp

def _softmax(x, axis=-1):
    return jax.nn.softmax(x, axis=axis)

def _gelu(x):
    return jax.nn.gelu(x, approximate=True)

def _silu(x):
    return jax.nn.silu(x)

def _sigmoid(x):
    return jax.nn.sigmoid(x)

def _layernorm(x, axis=-1, eps=1e-05):
    m = jnp.mean(x, axis=axis, keepdims=True)
    v = jnp.var(x, axis=axis, keepdims=True)
    return (x - m) / jnp.sqrt(v + eps)

def _scatter_add(tgt, idx, src, axis=0):
    return tgt.at[idx].add(src)

def _segment_sum(src, seg, n):
    return jax.ops.segment_sum(src, seg, n)
kernel_name = 'mk_xattn_ffn_d1_seqx_r8_d23dfc'

def setup_inputs(seed: int=0):
    np.random.seed(seed)
    _w = jnp.asarray

    def _rec_inputs():
        import jax
        import jax.numpy as jnp
        _rk = jax.random.key(seed)
        x = -0.0003929 + 0.9999 * jax.random.normal(jax.random.fold_in(_rk, 1), (32, 64, 512), jnp.float32)
        _lenS = 64 - jax.random.randint(jax.random.fold_in(_rk, 7), (32,), 0, max(1, 64 // 4) + 1, jnp.int32)
        _lenS2 = 64 - jax.random.randint(jax.random.fold_in(_rk, 8), (32,), 0, max(1, 64 // 4) + 1, jnp.int32)
        _ctx_4096P = jax.random.normal(jax.random.fold_in(_rk, 11), (32, 16, 512), jnp.float32)
        _ctx_4096c = jax.random.dirichlet(jax.random.fold_in(_rk, 511), 0.3 * jnp.ones((16,), jnp.float32), (32, 64))
        _ctx_4096t = jnp.einsum('bsk,bkd->bsd', _ctx_4096c, _ctx_4096P)
        _ctx_4096t = _ctx_4096t * jax.lax.rsqrt(jnp.mean(jnp.square(_ctx_4096t)) + 1e-12) * 0.953939
        ctx_4096 = 2.81802e-05 + 1.00001 * (_ctx_4096t + 0.3 * jax.random.normal(jax.random.fold_in(_rk, 611), (32, 64, 512), jnp.float32))
        return (x, ctx_4096)
    x, ctx_4096 = _rec_inputs()

    def _L0_xattn_setup():
        import jax, jax.numpy as jnp
        import numpy as np
        HID = 512
        NHEAD = 32
        NKV = 8
        HDIM = 128
        G = NHEAD // NKV
        key = jax.random.key(seed)
        ks = jax.random.split(key, 6)
        s = 0.02
        B, L = (2, 256)
        return {'query': jax.random.normal(ks[0], (B, L, HID), jnp.float32), 'kv': jax.random.normal(ks[1], (B, L, HID), jnp.float32), 'Wq': jax.random.normal(ks[2], (HID, NHEAD * HDIM), jnp.float32) * s, 'bq': jnp.zeros((NHEAD * HDIM,), jnp.float32), 'Wkv': jax.random.normal(ks[3], (HID, 2 * NKV * HDIM), jnp.float32) * s, 'bkv': jnp.zeros((2 * NKV * HDIM,), jnp.float32), 'Wo': jax.random.normal(ks[4], (NHEAD * HDIM, HID), jnp.float32) * s, 'bo': jnp.zeros((HID,), jnp.float32)}
    _L0_xattn_all = _L0_xattn_setup()
    _L0_xattn_in = {k: v for k, v in _L0_xattn_all.items() if k in ('Wq', 'bq', 'Wkv', 'bkv', 'Wo', 'bo')}
    del _L0_xattn_all

    def _L0_ffn_setup():
        import jax, jax.numpy as jnp
        import numpy as np
        HIDDEN = 512
        SPARSITY_RATIO = 0.1
        BLOCK_SIZE = max(1, int(HIDDEN * SPARSITY_RATIO * 2))

        def _block_diag_mask(h: int, block_size: int) -> jnp.ndarray:
            idx = jnp.arange(h) // block_size
            return idx[:, None] == idx[None, :]
        key = jax.random.key(seed)
        kx, kw = jax.random.split(key)
        x = jax.random.normal(kx, (8, 256, HIDDEN), dtype=jnp.float32)
        mask = _block_diag_mask(HIDDEN, BLOCK_SIZE)
        eye = jnp.eye(HIDDEN, dtype=jnp.float32)
        W = eye + 0.1 * jax.random.normal(kw, (HIDDEN, HIDDEN), dtype=jnp.float32)
        W = W * mask.astype(jnp.float32) + eye * (~mask).astype(jnp.float32)
        return {'x': x, 'W': W, 'mask': mask}
    _L0_ffn_all = _L0_ffn_setup()
    _L0_ffn_in = {k: v for k, v in _L0_ffn_all.items() if k in ('W', 'mask')}
    del _L0_ffn_all
    return {'x': x, 'ctx_4096': ctx_4096, 'L0_xattn_Wq': _L0_xattn_in['Wq'], 'L0_xattn_bq': _L0_xattn_in['bq'], 'L0_xattn_Wkv': _L0_xattn_in['Wkv'], 'L0_xattn_bkv': _L0_xattn_in['bkv'], 'L0_xattn_Wo': _L0_xattn_in['Wo'], 'L0_xattn_bo': _L0_xattn_in['bo'], 'L0_ffn_W': _L0_ffn_in['W'], 'L0_ffn_mask': _L0_ffn_in['mask']}

def reference(x, ctx_4096, L0_xattn_Wq, L0_xattn_bq, L0_xattn_Wkv, L0_xattn_bkv, L0_xattn_Wo, L0_xattn_bo, L0_ffn_W, L0_ffn_mask):
    import jax
    import jax.numpy as jnp

    def _L0_xattn_ref(query, kv, Wq, bq, Wkv, bkv, Wo, bo):
        import jax, jax.numpy as jnp
        import numpy as np
        HID = 512
        NHEAD = 32
        NKV = 8
        HDIM = 128
        G = NHEAD // NKV
        B, L, _ = query.shape
        Lk = kv.shape[1]
        scale = jnp.asarray(1.0 / np.sqrt(HDIM), query.dtype)
        q = (query @ Wq + bq).reshape(B, L, NKV, G, HDIM)
        k_, v_ = jnp.split(kv @ Wkv + bkv, 2, axis=-1)
        k = k_.reshape(B, Lk, NKV, HDIM)
        v = v_.reshape(B, Lk, NKV, HDIM)
        scores = jnp.einsum('blkgd,bmkd->bkglm', q, k) * scale
        attn = jax.nn.softmax(scores, axis=-1)
        o = jnp.einsum('bkglm,bmkd->blkgd', attn, v).reshape(B, L, NHEAD * HDIM)
        return o @ Wo + bo

    def _L0_ffn_ref(x, W, mask):
        import jax, jax.numpy as jnp
        import numpy as np
        HIDDEN = 512
        SPARSITY_RATIO = 0.1
        BLOCK_SIZE = max(1, int(HIDDEN * SPARSITY_RATIO * 2))

        def _block_diag_mask(h: int, block_size: int) -> jnp.ndarray:
            idx = jnp.arange(h) // block_size
            return idx[:, None] == idx[None, :]
        sparse_W = W * mask.astype(W.dtype)
        return jnp.einsum('bsh,oh->bso', x, sparse_W)
    x = x + _L0_xattn_ref(_layernorm(x, axis=-1), ctx_4096, L0_xattn_Wq, L0_xattn_bq, L0_xattn_Wkv, L0_xattn_bkv, L0_xattn_Wo, L0_xattn_bo)
    x = x + _L0_ffn_ref(_layernorm(x, axis=-1), L0_ffn_W, L0_ffn_mask)
    return x

_drawn_inputs = setup_inputs


def setup_inputs(seed=0):
    import zlib

    import numpy as np

    out = dict(_drawn_inputs(seed))
    spreads = {'L0_xattn_bq': (0.0, 0.8), 'L0_xattn_bkv': (0.0, 0.1), 'L0_xattn_bo': (0.0, 0.1)}
    factors = {}
    for name, (base, spread) in spreads.items():
        noise = np.random.default_rng([zlib.crc32(name.encode()), seed]).standard_normal(out[name].shape)
        drawn = base * np.exp(spread * noise) if base else spread * noise
        out[name] = jnp.asarray(drawn.astype(out[name].dtype))
    for name, factor in factors.items():
        out[name] = (out[name] * factor).astype(out[name].dtype)
    return out
```

```python
from contextlib import ExitStack

import concourse.bass as bass
from concourse import mybir

F32 = mybir.dt.float32
F32R = mybir.dt.float32r
U8 = mybir.dt.uint8
ALU = mybir.AluOpType
ACT = mybir.ActivationFunctionType
AX_X = mybir.AxisListType.X

P = 128
EPS = 1e-5


def xattn_ffn(nc, x, ctxT, wq, bqk, wkv, bv, wo, bo, ffn_wT, ffn_maskT, out):
    TOKENS, D = x.shape
    NKV, HD, NB = bqk.shape
    GQ = NB - 1
    L = 64
    KT = D // P
    HALVES = 2
    HT = TOKENS // HALVES
    GT = 512
    NG = HT // GT
    NT = GT // P
    HN = HT // P
    STEPS = NKV * NG
    KVW = NKV * HD
    SCALE = float(HD) ** -0.5
    assert HD == P and NG == 2 and NT == 4 and KT == 4 and GQ == 4

    with ExitStack() as ctx:
        def sb(name, shape, dt=F32):
            return ctx.enter_context(nc.sbuf_tensor(name, shape, dt))

        def sem(name):
            return ctx.enter_context(nc.semaphore(name))

        xT_hi = sb("xT_hi", [P, KT, HT], F32R)
        xT_lo = sb("xT_lo", [P, KT, HT], F32R)
        cT_hi = sb("cT_hi", [P, KT, HT], F32R)
        cT_lo = sb("cT_lo", [P, KT, HT], F32R)
        acc = sb("acc", [P, HN, D])
        wq_hi = sb("wq_hi", [P, KT, GQ * HD], F32R)
        wq_lo = sb("wq_lo", [P, KT, GQ * HD], F32R)
        wkv_hi = sb("wkv_hi", [P, 2, KT, HD], F32R)
        wkv_lo = sb("wkv_lo", [P, 2, KT, HD], F32R)
        wo_hi = sb("wo_hi", [P, GQ, D], F32R)
        wo_lo = sb("wo_lo", [P, GQ, D], F32R)
        wq_stage = sb("wq_stage", [P, KT, GQ * HD])
        wkv_stage = sb("wkv_stage", [P, 2, KT, HD])
        wo_stage = sb("wo_stage", [P, GQ, D])
        ctx_stage = sb("ctx_stage", [P, 2, GT])
        mask_stage = sb("mask_stage", [P, KT, D], U8)
        bqk_stage = sb("bqk_stage", [P, NB])
        bqk_now = sb("bqk_now", [P, NB])
        bv_stage = sb("bv_stage", [P, 1])
        bv_now = sb("bv_now", [P, 1])
        bo_all = sb("bo_all", [P, D])
        ident = sb("ident", [P, P])
        q_hi = sb("q_hi", [P, GT // L, GQ, L], F32R)
        q_lo = sb("q_lo", [P, GT // L, GQ, L], F32R)
        k_hi = sb("k_hi", [P, GT], F32R)
        k_lo = sb("k_lo", [P, GT], F32R)
        v_hi = sb("v_hi", [P, NT, HD], F32R)
        v_lo = sb("v_lo", [P, NT, HD], F32R)
        probs = sb("probs", [P, 2, 8, L])
        pT_hi = sb("pT_hi", [P, NT, 2 * P], F32R)
        pT_lo = sb("pT_lo", [P, NT, 2 * P], F32R)
        o_hi = sb("o_hi", [P, NT, GQ, 2, L], F32R)
        o_lo = sb("o_lo", [P, NT, GQ, 2, L], F32R)
        row_max = sb("row_max", [P, 16])
        row_sum = sb("row_sum", [P, 16])
        row_inv = sb("row_inv", [P, 16])
        xn = sb("xn", [P, 2, D])
        stats = sb("stats", [P, HN, 6])
        mean, gap = [sb(n, [P, HN]) for n in ("mean", "gap")]
        var, root, guess, square, rstd = [sb(n, [P, HN]) for n in ("var", "root", "guess", "square", "rstd")]

        ps = [ctx.enter_context(nc.psum_tensor(f"ps{b}", [P, 512], F32)) for b in range(2, 8)]
        ps01 = ctx.enter_context(nc.psum_tensor("ps01", [P, 2, 512], F32))

        def bank(b):
            return ps01[:, b, :] if b < 2 else ps[b - 2][:, :]

        BK, BQ, BV, BY, BO = 2, [3, 4, 5, 2], 6, [3, 4, 5, 7], [6, 7, 0, 1]
        BX, BF = [2, 3, 4, 5], [6, 7, 0, 1]

        qkv_loaded, qkv_hi_done, qkv_ready = sem("qkv_loaded"), sem("qkv_hi_done"), sem("qkv_ready")
        wo_loaded, wo_hi_done, wo_ready = sem("wo_loaded"), sem("wo_hi_done"), sem("wo_ready")
        bias_set = sem("bias_set")
        ffn_loaded, ffn_masked = sem("ffn_loaded"), sem("ffn_masked")
        ffn_hi_done, ffn_ready = sem("ffn_hi_done"), sem("ffn_ready")
        x_loaded = [sem(f"x_loaded{n}") for n in range(NG)]
        ctx_loaded = [sem(f"ctx_loaded{n}") for n in range(2)]
        ctx_hi_done, ctx_ready = sem("ctx_hi_done"), sem("ctx_ready")
        bo_loaded, ident_zero, ident_ready = sem("bo_loaded"), sem("ident_zero"), sem("ident_ready")
        bo_added = sem("bo_added")
        stats_done, aggr_done, var_done = sem("stats_done"), sem("aggr_done"), sem("var_done")
        root_done, newton, rstd_done = sem("root_done"), sem("newton"), sem("rstd_done")
        xn_done, xT_mm, xT_hi_done, xT_ready = sem("xn_done"), sem("xT_mm"), sem("xT_hi_done"), sem("xT_ready")
        k_mm, k_hi_done, k_ready = sem("k_mm"), sem("k_hi_done"), sem("k_ready")
        q_mm, q_hi_done, q_ready = sem("q_mm"), sem("q_hi_done"), sem("q_ready")
        v_mm, v_hi_done, v_ready = sem("v_mm"), sem("v_hi_done"), sem("v_ready")
        s_mm, max_done, shifted, exp_done = sem("s_mm"), sem("max_done"), sem("shifted"), sem("exp_done")
        sum_done, inv_done, probs_ready = sem("sum_done"), sem("inv_done"), sem("probs_ready")
        pT_mm, pT_hi_done, pT_ready = sem("pT_mm"), sem("pT_hi_done"), sem("pT_ready")
        o_mm, o_hi_done, o_ready = sem("o_mm"), sem("o_hi_done"), sem("o_ready")
        y_mm, y_added = sem("y_mm"), sem("y_added")
        f_mm, f_added, stored = sem("f_mm"), sem("f_added"), sem("stored")

        x_tiles = x.rearrange("(u n p) d -> u p n d", p=P, n=NT)
        out_tiles = out.rearrange("(t p) d -> t p d", p=P)
        ctx_tiles = ctxT.rearrange("(k p) (u t) -> k u p t", p=P, t=GT)
        wq_heads = wq.rearrange("(k p) (g n) -> g p k n", p=P, n=GQ * HD)
        wk_heads = wkv[:, 0:KVW].rearrange("(k p) (g n) -> g p k n", p=P, n=HD)
        wv_heads = wkv[:, KVW:2 * KVW].rearrange("(k p) (g n) -> g p k n", p=P, n=HD)
        wo_heads = wo.rearrange("(g h p) n -> g p h n", p=P, h=GQ)

        def f32(ap):
            return ap.bitcast(F32)

        block = ctx.enter_context(nc.Block())

        @block.sync
        def _(sp):
            def load_qkv(g, half):
                if not (isinstance(g, int) and g == 0 and half == 0):
                    sp.wait_ge(qkv_ready, half * NKV + g)
                sp.dma_start(wkv_stage[:, 0, :, :], wk_heads[g]).then_inc(qkv_loaded, 16)
                sp.dma_start(wq_stage[:, :, :], wq_heads[g]).then_inc(qkv_loaded, 16)
                sp.dma_start(wkv_stage[:, 1, :, :], wv_heads[g]).then_inc(qkv_loaded, 16)
                sp.dma_start(bqk_stage[:, :], bqk[g]).then_inc(qkv_loaded, 16)

            def load_wo(g, half):
                if not (isinstance(g, int) and g == 0):
                    sp.wait_ge(wo_ready, half * NKV + g)
                elif half:
                    sp.wait_ge(ffn_ready, half)
                sp.dma_start(wo_stage[:, :, :], wo_heads[g]).then_inc(wo_loaded, 16)
                sp.dma_start(bv_stage[:, :], bv[g]).then_inc(wo_loaded, 16)

            def load_ctx(half, n):
                for k in range(KT):
                    c = n * KT + k
                    if half or c >= 2:
                        sp.wait_ge(ctx_ready, half * (NG * KT) + c - 1)
                    sp.dma_start(ctx_stage[:, c % 2, :], ctx_tiles[k, half * NG + n]).then_inc(ctx_loaded[c % 2], 16)

            for half in range(HALVES):
                load_qkv(0, half)
                for n in range(NG):
                    if half:
                        sp.wait_ge(stored, half * (16 * HN))
                    sp.dma_start(acc[:, n * NT:(n + 1) * NT, :], x_tiles[half * NG + n]).then_inc(x_loaded[n], 16)
                    load_ctx(half, n)
                load_wo(0, half)
                with sp.Fori(1, NKV) as g:
                    load_qkv(g, half)
                    load_wo(g, half)
                sp.wait_ge(wo_ready, half * NKV + NKV)
                sp.dma_start(wo_stage[:, :, :], ffn_wT.rearrange("(k p) o -> p k o", p=P)).then_inc(ffn_loaded, 16)
                sp.dma_start(mask_stage[:, :, :], ffn_maskT.rearrange("(k p) o -> p k o", p=P)).then_inc(ffn_loaded, 16)
            sp.wait_ge(stored, 16 * HN * HALVES)

        @block.gpsimd
        def _(pool):
            pool.dma_start(bo_all[:, :], bo.broadcast_to([P, D])).then_inc(bo_loaded, 16)
            nc.gpsimd.memset(ident[:, :], 0.0).then_inc(ident_zero, 1)
            pool.wait_ge(ident_zero, 1)
            nc.gpsimd.affine_select(out=ident[:, :], in_=ident[:, :], compare_op=ALU.not_equal, fill=1.0,
                                    base=0, pattern=[[-1, P]], channel_multiplier=1).then_inc(ident_ready, 1)

            def qkv_parts(G):
                pool.wait_ge(qkv_hi_done, G * 2 + 1)
                nc.gpsimd.tensor_tensor(wkv_lo[:, :, :, :], wkv_stage[:, :, :, :], f32(wkv_hi[:, :, :, :]), ALU.subtract)
                pool.wait_ge(qkv_hi_done, G * 2 + 2)
                nc.gpsimd.tensor_tensor(wq_lo[:, :, :], wq_stage[:, :, :], f32(wq_hi[:, :, :]),
                                        ALU.subtract).then_inc(qkv_ready, 1)

            def wo_parts(G):
                pool.wait_ge(wo_hi_done, G + 1)
                nc.gpsimd.tensor_tensor(wo_lo[:, :, :], wo_stage[:, :, :], f32(wo_hi[:, :, :]),
                                        ALU.subtract).then_inc(wo_ready, 1)

            def ctx_parts(half, n):
                for k in range(KT):
                    c = n * KT + k
                    pool.wait_ge(ctx_hi_done, half * (NG * KT) + c + 1)
                    nc.gpsimd.tensor_tensor(cT_lo[:, k, n * GT:(n + 1) * GT], ctx_stage[:, c % 2, :],
                                            f32(cT_hi[:, k, n * GT:(n + 1) * GT]), ALU.subtract).then_inc(ctx_ready, 1)

            pool.wait_ge(bo_loaded, 16)
            with pool.Fori(0, HALVES) as half:
                qkv_parts(half * NKV)
                for n in range(NG):
                    ctx_parts(half, n)
                for n in range(NG):
                    pool.wait_ge(xn_done, half * 16 + (n + 1) * NT)
                    for j in range(NT):
                        t = n * NT + j
                        last = nc.gpsimd.tensor_tensor(acc[:, t, :], acc[:, t, :], bo_all[:, :], ALU.add)
                    last.then_inc(bo_added, 1)
                wo_parts(half * NKV)
                with pool.Fori(1, NKV) as g:
                    qkv_parts(half * NKV + g)
                    wo_parts(half * NKV + g)
                pool.wait_ge(ffn_hi_done, half + 1)
                nc.gpsimd.tensor_tensor(wo_lo[:, :, :], wo_stage[:, :, :], f32(wo_hi[:, :, :]),
                                        ALU.subtract).then_inc(ffn_ready, 1)

        @block.scalar
        def _(act):
            def copy(o, i):
                return nc.scalar.activation(o, i, ACT.Identity)

            def qkv_hi_parts(G):
                act.wait_ge(qkv_loaded, G * 64 + 64)
                copy(bqk_now[:, :], bqk_stage[:, :]).then_inc(bias_set, 1)
                copy(wkv_hi[:, :, :, :], wkv_stage[:, :, :, :]).then_inc(qkv_hi_done, 1)
                copy(wq_hi[:, :, :], wq_stage[:, :, :]).then_inc(qkv_hi_done, 1)

            def wo_hi_part(G):
                act.wait_ge(wo_loaded, G * 32 + 32)
                copy(bv_now[:, :], bv_stage[:, :]).then_inc(bias_set, 1)
                copy(wo_hi[:, :, :], wo_stage[:, :, :]).then_inc(wo_hi_done, 1)

            def ctx_hi_parts(half, n):
                for k in range(KT):
                    c = n * KT + k
                    act.wait_ge(ctx_loaded[c % 2], half * (16 * NG * KT // 2) + 16 * (c // 2 + 1))
                    copy(cT_hi[:, k, n * GT:(n + 1) * GT], ctx_stage[:, c % 2, :]).then_inc(ctx_hi_done, 1)

            def roots(B):
                act.wait_ge(var_done, B + 1)
                nc.scalar.activation(root[:, :], var[:, :], ACT.Sqrt).then_inc(root_done, 1)

            def xT_hi_parts(B, n):
                for j in range(NT):
                    act.wait_ge(xT_mm, B * NT + (j + 1))
                    t = n * NT + j
                    copy(xT_hi[:, :, t * P:(t + 1) * P],
                         bank(BX[j]).rearrange("p (k t) -> p k t", k=KT)).then_inc(xT_hi_done, 1)

            def k_hi_part(S, G, n):
                act.wait_ge(k_mm, S + 1)
                if n == 0:
                    act.wait_ge(bias_set, G * 2 + 1)
                nc.scalar.activation(k_hi[:, :], bank(BK), ACT.Identity, bias=bqk_now[:, GQ:NB]).then_inc(k_hi_done, 1)

            def q_hi_part(S, h):
                act.wait_ge(q_mm, S * GQ + (h + 1))
                nc.scalar.activation(q_hi[:, :, h, :], bank(BQ[h]).rearrange("p (b l) -> p b l", l=L),
                                     ACT.Identity, bias=bqk_now[:, h:h + 1]).then_inc(q_hi_done, 1)

            def v_hi_part(S):
                act.wait_ge(v_mm, S + 1)
                copy(v_hi[:, :, :], bank(BV).rearrange("p (t d) -> p t d", d=HD)).then_inc(v_hi_done, 1)

            def exps(S):
                for i in range(2):
                    act.wait_ge(shifted, S * 2 + (i + 1))
                    nc.scalar.activation(probs[:, i, :, :], probs[:, i, :, :], ACT.Exp, scale=SCALE).then_inc(exp_done, 1)

            def pT_hi_parts(S):
                for i in range(2):
                    act.wait_ge(pT_mm, S * 2 + (i + 1))
                    copy(pT_hi[:, 2 * i:2 * i + 2, :], ps01[:, i, :].rearrange("p (t q) -> p t q", t=2)).then_inc(pT_hi_done, 1)

            def step(S, G, n, more):
                if more:
                    k_hi_part(S + 1, G + 1, 1 - n)
                    q_hi_part(S + 1, 0)
                    q_hi_part(S + 1, 1)
                if n == 0:
                    wo_hi_part(G)
                    act.wait_ge(bias_set, G * 2 + 2)
                for i in range(4):
                    r, b = i // 2, i % 2
                    act.wait_ge(o_mm, S * 4 + (i + 1))
                    nc.scalar.activation(o_hi[:, 2 * r:2 * r + 2, :, b, :].rearrange("p t h l -> p (t h) l"),
                                         bank(BO[i]).rearrange("p (x l) -> p x l", l=L),
                                         ACT.Identity, bias=bv_now[:, 0:1]).then_inc(o_hi_done, 1)
                if more:
                    q_hi_part(S + 1, 2)
                    q_hi_part(S + 1, 3)
                    v_hi_part(S + 1)
                    exps(S + 1)
                    if n == 0 and more != "last":
                        qkv_hi_parts(G + 1)
                    pT_hi_parts(S + 1)

            with act.Fori(0, HALVES) as half:
                S0 = half * STEPS
                G0 = half * NKV
                qkv_hi_parts(G0)
                ctx_hi_parts(half, 0)
                roots(half * 2)
                xT_hi_parts(half * 4, 0)
                k_hi_part(S0, G0, 0)
                for h in range(GQ):
                    q_hi_part(S0, h)
                v_hi_part(S0)
                exps(S0)
                ctx_hi_parts(half, 1)
                xT_hi_parts(half * 4 + 1, 1)
                pT_hi_parts(S0)
                with act.Fori(0, NKV - 1) as g:
                    step(S0 + g * NG, G0 + g, 0, True)
                    step(S0 + g * NG + 1, G0 + g, 1, True)
                step(S0 + (STEPS - 2), G0 + (NKV - 1), 0, "last")
                step(S0 + (STEPS - 1), G0 + (NKV - 1), 1, False)
                roots(half * 2 + 1)
                act.wait_ge(y_mm, half * (STEPS * NT) + STEPS * NT)
                act.wait_ge(ffn_masked, half + 1)
                copy(wo_hi[:, :, :], wo_stage[:, :, :]).then_inc(ffn_hi_done, 1)
                xT_hi_parts(half * 4 + 2, 0)
                xT_hi_parts(half * 4 + 3, 1)
                for t in range(HN):
                    act.wait_ge(f_added, half * HN + (t + 1))
                    act.dma_start(out_tiles[half * HN + t], acc[:, t, :]).then_inc(stored, 16)

        @block.vector
        def _(dve):
            def low(o, psum, hi, bias=None):
                if bias is None:
                    return nc.vector.tensor_tensor(o, psum, f32(hi), ALU.subtract)
                return nc.vector.scalar_tensor_tensor(out=o, in0=psum, scalar=bias, in1=f32(hi),
                                                      op0=ALU.add, op1=ALU.subtract)

            def norm_stats(B):
                for t in range(HN):
                    last = nc.vector.bn_stats(stats[:, t, :], acc[:, t, :])
                last.then_inc(stats_done, 1)
                dve.wait_ge(stats_done, B + 1)
                nc.vector.tensor_tensor(mean[:, :], stats[:, :, 1], stats[:, :, 4], ALU.add)
                nc.vector.tensor_tensor(gap[:, :], stats[:, :, 1], stats[:, :, 4], ALU.subtract)
                nc.vector.tensor_tensor(var[:, :], stats[:, :, 2], stats[:, :, 5], ALU.add).then_inc(aggr_done, 1)
                dve.wait_ge(aggr_done, B * 2 + 1)
                nc.vector.tensor_scalar(mean[:, :], mean[:, :], 0.5, None, ALU.mult)
                nc.vector.tensor_tensor(gap[:, :], gap[:, :], gap[:, :], ALU.mult)
                nc.vector.tensor_scalar(var[:, :], var[:, :], 1.0 / D, EPS, ALU.mult, ALU.add).then_inc(aggr_done, 1)
                dve.wait_ge(aggr_done, B * 2 + 2)
                nc.vector.scalar_tensor_tensor(out=var[:, :], in0=gap[:, :], scalar=0.25, in1=var[:, :],
                                               op0=ALU.mult, op1=ALU.add).then_inc(var_done, 1)
                dve.wait_ge(root_done, B + 1)
                nc.vector.reciprocal(guess[:, :], root[:, :]).then_inc(newton, 1)
                dve.wait_ge(newton, B * 4 + 1)
                nc.vector.tensor_tensor(square[:, :], guess[:, :], guess[:, :], ALU.mult).then_inc(newton, 1)
                dve.wait_ge(newton, B * 4 + 2)
                nc.vector.tensor_tensor(square[:, :], square[:, :], var[:, :], ALU.mult).then_inc(newton, 1)
                dve.wait_ge(newton, B * 4 + 3)
                nc.vector.tensor_scalar(square[:, :], square[:, :], -0.5, 1.5, ALU.mult, ALU.add).then_inc(newton, 1)
                dve.wait_ge(newton, B * 4 + 4)
                nc.vector.tensor_tensor(rstd[:, :], guess[:, :], square[:, :], ALU.mult).then_inc(rstd_done, 1)
                dve.wait_ge(rstd_done, B + 1)

            def normed(B, n, j):
                nc.vector.tensor_scalar(xn[:, j % 2, :], acc[:, n * NT + j, :], mean[:, n * NT + j:n * NT + j + 1],
                                        rstd[:, n * NT + j:n * NT + j + 1],
                                        ALU.subtract, ALU.mult).then_inc(xn_done, 1)

            def xT_lo_part(B, n, j):
                dve.wait_ge(xT_hi_done, B * NT + (j + 1))
                t = n * NT + j
                low(xT_lo[:, :, t * P:(t + 1) * P], bank(BX[j]).rearrange("p (k t) -> p k t", k=KT),
                    xT_hi[:, :, t * P:(t + 1) * P]).then_inc(xT_ready, 1)

            def norm_group(B, n):
                normed(B, n, 0)
                normed(B, n, 1)
                for j in range(NT):
                    xT_lo_part(B, n, j)
                    if j + 2 < NT:
                        normed(B, n, j + 2)

            def k_lo_part(S):
                dve.wait_ge(k_hi_done, S + 1)
                low(k_lo[:, :], bank(BK), k_hi[:, :], bqk_now[:, GQ:NB]).then_inc(k_ready, 1)

            def q_lo_part(S, h):
                dve.wait_ge(q_hi_done, S * GQ + (h + 1))
                low(q_lo[:, :, h, :], bank(BQ[h]).rearrange("p (b l) -> p b l", l=L),
                    q_hi[:, :, h, :], bqk_now[:, h:h + 1]).then_inc(q_ready, 1)

            def v_lo_part(S):
                dve.wait_ge(v_hi_done, S + 1)
                low(v_lo[:, :, :], bank(BV).rearrange("p (t d) -> p t d", d=HD), v_hi[:, :, :]).then_inc(v_ready, 1)

            def softmax(S):
                dve.wait_ge(s_mm, S + 1)
                nc.vector.tensor_reduce(row_max[:, :], ps01[:, :, :].rearrange("p i (x m) -> p (i x) m", m=L),
                                        AX_X, ALU.max).then_inc(max_done, 1)
                dve.wait_ge(max_done, S + 1)
                for i in range(2):
                    nc.vector.tensor_tensor(probs[:, i, :, :], ps01[:, i, :].rearrange("p (x m) -> p x m", m=L),
                                            row_max[:, 8 * i:8 * i + 8].unsqueeze(2).broadcast_to([P, 8, L]),
                                            ALU.subtract).then_inc(shifted, 1)
                for i in range(2):
                    dve.wait_ge(exp_done, S * 2 + (i + 1))
                    last = nc.vector.tensor_reduce(row_sum[:, 8 * i:8 * i + 8], probs[:, i, :, :], AX_X, ALU.add)
                last.then_inc(sum_done, 1)
                dve.wait_ge(sum_done, S + 1)
                nc.vector.reciprocal(row_inv[:, :], row_sum[:, :]).then_inc(inv_done, 1)
                dve.wait_ge(inv_done, S + 1)
                for i in range(2):
                    nc.vector.tensor_tensor(probs[:, i, :, :], probs[:, i, :, :],
                                            row_inv[:, 8 * i:8 * i + 8].unsqueeze(2).broadcast_to([P, 8, L]),
                                            ALU.mult).then_inc(probs_ready, 1)

            def pT_lo_parts(S):
                for i in range(2):
                    dve.wait_ge(pT_hi_done, S * 2 + (i + 1))
                    low(pT_lo[:, 2 * i:2 * i + 2, :], ps01[:, i, :].rearrange("p (t q) -> p t q", t=2),
                        pT_hi[:, 2 * i:2 * i + 2, :]).then_inc(pT_ready, 1)

            def step(S, n, more):
                if more:
                    k_lo_part(S + 1)
                    q_lo_part(S + 1, 0)
                    q_lo_part(S + 1, 1)
                for i in range(4):
                    r, b = i // 2, i % 2
                    dve.wait_ge(o_hi_done, S * 4 + (i + 1))
                    low(o_lo[:, 2 * r:2 * r + 2, :, b, :].rearrange("p t h l -> p (t h) l"),
                        bank(BO[i]).rearrange("p (x l) -> p x l", l=L),
                        o_hi[:, 2 * r:2 * r + 2, :, b, :].rearrange("p t h l -> p (t h) l"),
                        bv_now[:, 0:1]).then_inc(o_ready, 1)
                if more:
                    q_lo_part(S + 1, 2)
                    q_lo_part(S + 1, 3)
                    v_lo_part(S + 1)
                    softmax(S + 1)
                for j in range(NT):
                    t = n * NT + j
                    dve.wait_ge(y_mm, S * NT + (j + 1))
                    nc.vector.tensor_tensor(acc[:, t, :], bank(BY[j]), acc[:, t, :], ALU.add).then_inc(y_added, 1)
                if more:
                    pT_lo_parts(S + 1)

            with dve.Fori(0, HALVES) as half:
                S0 = half * STEPS
                for n in range(NG):
                    dve.wait_ge(x_loaded[n], half * 16 + 16)
                norm_stats(half * 2)
                norm_group(half * 4, 0)
                k_lo_part(S0)
                for h in range(GQ):
                    q_lo_part(S0, h)
                v_lo_part(S0)
                softmax(S0)
                norm_group(half * 4 + 1, 1)
                dve.wait_ge(bo_added, half * NG + NG)
                pT_lo_parts(S0)
                with dve.Fori(0, NKV - 1) as g:
                    step(S0 + g * NG, 0, True)
                    step(S0 + g * NG + 1, 1, True)
                step(S0 + (STEPS - 2), 0, True)
                step(S0 + (STEPS - 1), 1, False)
                dve.wait_ge(ffn_loaded, half * 32 + 32)
                nc.vector.tensor_tensor(wo_stage[:, :, :], wo_stage[:, :, :], mask_stage[:, :, :],
                                        ALU.mult).then_inc(ffn_masked, 1)
                dve.wait_ge(y_added, half * (STEPS * NT) + STEPS * NT)
                norm_stats(half * 2 + 1)
                for n in range(NG):
                    norm_group(half * 4 + 2 + n, n)
                for t in range(HN):
                    dve.wait_ge(f_mm, half * HN + (t + 1))
                    nc.vector.tensor_tensor(acc[:, t, :], bank(BF[t % 4]), acc[:, t, :], ALU.add).then_inc(f_added, 1)

        @block.tensor
        def _(pe):
            def product(o, pairs, first=True, last=True):
                for n, ((a_hi, a_lo), (b_hi, b_lo)) in enumerate(pairs):
                    nc.tensor.matmul(o, a_hi, b_hi, start=(n == 0), stop=False)
                    nc.tensor.matmul(o, a_hi, b_lo, start=False, stop=False)
                    mm = nc.tensor.matmul(o, a_lo, b_hi, start=False, stop=(n == len(pairs) - 1))
                return mm

            def turn_x(B):
                for j in range(NT):
                    pe.wait_ge(xn_done, B * NT + (j + 1))
                    for k in range(KT):
                        mm = nc.tensor.transpose(bank(BX[j])[:, k * P:(k + 1) * P], xn[:, j % 2, k * P:(k + 1) * P],
                                                 ident[:, :])
                    mm.then_inc(xT_mm, 1)

            def proj_k(S, n):
                product(bank(BK), [((wkv_hi[:, 0, k, :], wkv_lo[:, 0, k, :]),
                                    (cT_hi[:, k, n * GT:(n + 1) * GT], cT_lo[:, k, n * GT:(n + 1) * GT]))
                                   for k in range(KT)]).then_inc(k_mm, 1)

            def proj_q(S, n, h):
                product(bank(BQ[h]), [((wq_hi[:, k, h * HD:(h + 1) * HD], wq_lo[:, k, h * HD:(h + 1) * HD]),
                                       (xT_hi[:, k, n * GT:(n + 1) * GT], xT_lo[:, k, n * GT:(n + 1) * GT]))
                                      for k in range(KT)]).then_inc(q_mm, 1)

            def proj_v(S, n):
                for j in range(NT):
                    t = slice(n * GT + j * P, n * GT + (j + 1) * P)
                    mm = product(bank(BV)[:, j * HD:(j + 1) * HD],
                                 [((cT_hi[:, k, t], cT_lo[:, k, t]), (wkv_hi[:, 1, k, :], wkv_lo[:, 1, k, :]))
                                  for k in range(KT)])
                mm.then_inc(v_mm, 1)

            def scores(S):
                for j in range(NT):
                    for hp in range(2):
                        for b in range(2):
                            c = (j % 2) * 4 + hp * 2 + b
                            q = (2 * j + b, slice(2 * hp, 2 * hp + 2))
                            k = slice((2 * j + b) * L, (2 * j + b + 1) * L)
                            mm = product(ps01[:, j // 2, c * L:(c + 1) * L],
                                         [((q_hi[:, q[0], q[1], :].rearrange("p h l -> p (h l)"),
                                            q_lo[:, q[0], q[1], :].rearrange("p h l -> p (h l)")),
                                           (k_hi[:, k], k_lo[:, k]))])
                mm.then_inc(s_mm, 1)

            def turn_probs(S):
                for i in range(2):
                    pe.wait_ge(probs_ready, S * 2 + (i + 1))
                    for c in range(4):
                        mm = nc.tensor.transpose(ps01[:, i, c * P:(c + 1) * P],
                                                 probs[:, i, 2 * c:2 * c + 2, :].rearrange("p b m -> p (b m)"),
                                                 ident[:, :])
                    mm.then_inc(pT_mm, 1)

            def attend(S, r):
                for j in (2 * r, 2 * r + 1):
                    for a, w in ((v_hi, pT_hi), (v_hi, pT_lo), (v_lo, pT_hi)):
                        for b in range(2):
                            o = bank(BO[2 * r + b])[:, (j % 2) * 256:(j % 2) * 256 + 256]
                            mm = nc.tensor.matmul(o, a[b * L:(b + 1) * L, j, :], w[b * L:(b + 1) * L, j, :],
                                                  start=(a is v_hi and w is pT_hi), stop=(a is v_lo))
                            if j % 2 == 1 and a is v_lo:
                                mm.then_inc(o_mm, 1)

            def project_out(S, n):
                for j in range(NT):
                    product(bank(BY[j]), [((o_hi[:, j, h, :, :].rearrange("p b l -> p (b l)"),
                                            o_lo[:, j, h, :, :].rearrange("p b l -> p (b l)")),
                                           (wo_hi[:, h, :], wo_lo[:, h, :])) for h in range(GQ)]).then_inc(y_mm, 1)

            def step(S, G, n, more):
                if more:
                    if n == 1:
                        pe.wait_ge(qkv_ready, G + 2)
                    pe.wait_ge(q_ready, S * GQ + GQ)
                    proj_k(S + 1, 1 - n)
                pe.wait_ge(pT_ready, S * 2 + 2)
                if more:
                    proj_q(S + 1, 1 - n, 0)
                    proj_q(S + 1, 1 - n, 1)
                pe.wait_ge(v_ready, S + 1)
                attend(S, 0)
                attend(S, 1)
                if more:
                    proj_q(S + 1, 1 - n, 2)
                    pe.wait_ge(k_ready, S + 2)
                    proj_q(S + 1, 1 - n, 3)
                    pe.wait_ge(o_ready, S * 4 + 1)
                    proj_v(S + 1, 1 - n)
                pe.wait_ge(o_ready, S * 4 + 4)
                if more:
                    pe.wait_ge(q_ready, S * GQ + 2 * GQ)
                    scores(S + 1)
                if n == 0:
                    pe.wait_ge(wo_ready, G + 1)
                project_out(S, n)
                if more:
                    turn_probs(S + 1)

            pe.wait_ge(ident_ready, 1)
            with pe.Fori(0, HALVES) as half:
                S0 = half * STEPS
                G0 = half * NKV
                turn_x(half * 4)
                pe.wait_ge(qkv_ready, G0 + 1)
                pe.wait_ge(ctx_ready, half * (NG * KT) + KT)
                pe.wait_ge(xT_ready, half * 16 + NT)
                proj_k(S0, 0)
                for h in range(GQ):
                    if h == GQ - 1:
                        pe.wait_ge(k_ready, S0 + 1)
                    proj_q(S0, 0, h)
                proj_v(S0, 0)
                pe.wait_ge(q_ready, S0 * GQ + GQ)
                scores(S0)
                turn_x(half * 4 + 1)
                pe.wait_ge(xT_ready, half * 16 + 2 * NT)
                pe.wait_ge(ctx_ready, half * (NG * KT) + 2 * KT)
                turn_probs(S0)
                with pe.Fori(0, NKV - 1) as g:
                    step(S0 + g * NG, G0 + g, 0, True)
                    step(S0 + g * NG + 1, G0 + g, 1, True)
                step(S0 + (STEPS - 2), G0 + (NKV - 1), 0, True)
                step(S0 + (STEPS - 1), G0 + (NKV - 1), 1, False)
                turn_x(half * 4 + 2)
                turn_x(half * 4 + 3)
                pe.wait_ge(ffn_ready, half + 1)
                pe.wait_ge(xT_ready, half * 16 + 16)
                for t in range(HN):
                    if t >= 4:
                        pe.wait_ge(f_added, half * HN + (t - 3))
                    product(bank(BF[t % 4]), [((xT_hi[:, k, t * P:(t + 1) * P], xT_lo[:, k, t * P:(t + 1) * P]),
                                               (wo_hi[:, k, :], wo_lo[:, k, :])) for k in range(KT)]).then_inc(f_mm, 1)


def kernel(x, ctx_4096, L0_xattn_Wq, L0_xattn_bq, L0_xattn_Wkv, L0_xattn_bkv, L0_xattn_Wo, L0_xattn_bo,
           L0_ffn_W, L0_ffn_mask):
    import numpy as np
    import concourse.bacc as bacc
    from concourse.bass_utils import run_bass_kernel_spmd

    B, S, D = x.shape
    HD = 128
    heads = np.asarray(L0_xattn_bq).reshape(8, 4, HD)
    kv_bias = np.asarray(L0_xattn_bkv).reshape(2, 8, HD)
    arrays = {
        "x": np.ascontiguousarray(np.asarray(x).reshape(B * S, D)),
        "ctxT": np.ascontiguousarray(np.asarray(ctx_4096).reshape(B * S, D).T),
        "wq": np.ascontiguousarray(L0_xattn_Wq),
        "bqk": np.ascontiguousarray(np.concatenate([heads, kv_bias[0][:, None]], axis=1).transpose(0, 2, 1)),
        "wkv": np.ascontiguousarray(L0_xattn_Wkv),
        "bv": np.ascontiguousarray(kv_bias[1][:, :, None]),
        "wo": np.ascontiguousarray(L0_xattn_Wo),
        "bo": np.ascontiguousarray(np.asarray(L0_xattn_bo)[None, :]),
        "ffn_wT": np.ascontiguousarray(np.asarray(L0_ffn_W).T),
        "ffn_maskT": np.ascontiguousarray(np.asarray(L0_ffn_mask).T),
    }
    nc = bacc.Bacc("TRN2", target_bir_lowering=False, num_devices=1)
    args = {n: nc.dram_tensor(n, a.shape, mybir.dt.from_np(a.dtype), kind="ExternalInput").ap() for n, a in arrays.items()}
    out = nc.dram_tensor("out", (B * S, D), F32, kind="ExternalOutput").ap()
    xattn_ffn(nc, out=out, **args)
    r = run_bass_kernel_spmd(nc, [arrays], core_ids=[0])
    return r.results[0]["out"].reshape(B, S, D)
```

```python
from contextlib import ExitStack

import concourse.bass as bass
from concourse import mybir

F32 = mybir.dt.float32
F32R = mybir.dt.float32r
U8 = mybir.dt.uint8
ALU = mybir.AluOpType
ACT = mybir.ActivationFunctionType
AX_X = mybir.AxisListType.X

P = 128
EPS = 1e-5


def xattn_ffn(nc, x, ctxT, wq, bqkv, wkv, wo, bo, ffn_wT, ffn_maskT, out):
    TOKENS, D = x.shape
    NKV, HD, NB = bqkv.shape
    GQ = NB - 2
    L = 64
    KT = D // P
    HALVES = 2
    HT = TOKENS // HALVES
    GT = 512
    NG = HT // GT
    NT = GT // P
    HN = HT // P
    STEPS = NKV * NG
    KVW = NKV * HD
    SCALE = float(HD) ** -0.5
    FFN_ORDER = [0, 2, 3, 1]
    assert HD == P and HALVES == 2 and NG == 2 and NT == 4 and KT == 4 and GQ == 4 and D == GQ * HD

    with ExitStack() as ctx:
        def sb(name, shape, dt=F32):
            return ctx.enter_context(nc.sbuf_tensor(name, shape, dt))

        def sem(name):
            return ctx.enter_context(nc.semaphore(name))

        xT_hi = sb("xT_hi", [P, KT, HT], F32R)
        xT_lo = sb("xT_lo", [P, KT, HT], F32R)
        cT_hi = sb("cT_hi", [P, KT, HT], F32R)
        cT_lo = sb("cT_lo", [P, KT, HT], F32R)
        acc = sb("acc", [P, HN, D])
        wq_hi = sb("wq_hi", [P, KT, GQ * HD], F32R)
        wq_lo = sb("wq_lo", [P, KT, GQ * HD], F32R)
        wkv_hi = sb("wkv_hi", [P, 2, KT, HD], F32R)
        wkv_lo = sb("wkv_lo", [P, 2, KT, HD], F32R)
        wo_hi = sb("wo_hi", [P, GQ, D], F32R)
        wo_lo = sb("wo_lo", [P, GQ, D], F32R)
        wq_stage = sb("wq_stage", [P, KT, GQ * HD])
        wkv_stage = sb("wkv_stage", [P, 2, KT, HD])
        wo_stage = sb("wo_stage", [P, GQ, D])
        ctx_stage = sb("ctx_stage", [P, 2, GT])
        x_stage = sb("x_stage", [P, NT, D])
        mask_stage = ctx_stage[:, :, :].bitcast(U8).rearrange("p i b -> p (i b)")[:, 0:KT * D].rearrange(
            "p (k o) -> p k o", k=KT)
        bias_stage = sb("bias_stage", [P, NB])
        bias_now = sb("bias_now", [P, NB])
        bo_all = sb("bo_all", [P, D])
        ident = sb("ident", [P, P])
        q_hi = sb("q_hi", [P, GT // L, GQ, L], F32R)
        q_lo = sb("q_lo", [P, GT // L, GQ, L], F32R)
        k_parts = sb("k_parts", [P, GT // L, 2, L], F32R)
        v_hi = sb("v_hi", [P, NT, HD], F32R)
        v_lo = sb("v_lo", [P, NT, HD], F32R)
        probs = sb("probs", [P, 2, 8, L])
        vT = probs[:, 0, :, :].rearrange("p x m -> p (x m)")
        pT_hi = sb("pT_hi", [P, NT, 2 * P], F32R)
        pT_lo = sb("pT_lo", [P, NT, 2 * P], F32R)
        o_hi = sb("o_hi", [P, NT, GQ, 2, L], F32R)
        o_lo = sb("o_lo", [P, NT, GQ, 2, L], F32R)
        row_max = sb("row_max", [P, 16])
        row_sum = sb("row_sum", [P, 16])
        row_inv = sb("row_inv", [P, 16])
        stats = sb("stats", [P, NT, 6])
        mean, gap, var, root, guess, square, rstd = [
            sb(n, [P, NT]) for n in ("mean", "gap", "var", "root", "guess", "square", "rstd")]

        ps01 = ctx.enter_context(nc.psum_tensor("ps01", [P, 2, 512], F32))
        ps = [ctx.enter_context(nc.psum_tensor(f"ps{b}", [P, 512], F32)) for b in range(2, 6)]
        ps67 = ctx.enter_context(nc.psum_tensor("ps67", [P, 2, 512], F32))

        def bank(b):
            return ps01[:, b, :] if b < 2 else ps67[:, b - 6, :] if b >= 6 else ps[b - 2][:, :]

        B_K, B_Q, B_O, B_VT, B_V = 2, [3, 4, 2, 3], [6, 7, 0, 1], 5, 4
        S_BANKS, B_Y, B_X = [ps01, ps67], [5, 2, 3, 4], [6, 7, 5, 4]
        B_F = [2, 3, 0, 1]

        qkv_loaded, qkv_hi_done, qkv_ready = sem("qkv_loaded"), sem("qkv_hi_done"), sem("qkv_ready")
        wo_loaded, wo_hi_done, wo_ready = sem("wo_loaded"), sem("wo_hi_done"), sem("wo_ready")
        kv_loaded, bias_set = sem("kv_loaded"), sem("bias_set")
        kv_ready = sem("kv_ready")
        ffn_loaded, ffn_masked = sem("ffn_loaded"), sem("ffn_masked")
        ffn_hi_done, ffn_ready = sem("ffn_hi_done"), sem("ffn_ready")
        x_loaded, acc_loaded, acc_ready = sem("x_loaded"), sem("acc_loaded"), sem("acc_ready")
        ctx_loaded = [sem(f"ctx_loaded{n}") for n in range(2)]
        ctx_hi_done, ctx_ready = sem("ctx_hi_done"), sem("ctx_ready")
        bo_loaded, ident_zero, ident_ready = sem("bo_loaded"), sem("ident_zero"), sem("ident_ready")
        spilled, rest_loaded, stored = sem("spilled"), sem("rest_loaded"), sem("stored")
        stats_done, aggr_done, var_done = sem("stats_done"), sem("aggr_done"), sem("var_done")
        root_done, newton, rstd_done = sem("root_done"), sem("newton"), sem("rstd_done")
        xn_done, xT_mm, xT_hi_done, xT_ready = sem("xn_done"), sem("xT_mm"), sem("xT_hi_done"), sem("xT_ready")
        k_mm, k_hi_done, k_ready = sem("k_mm"), sem("k_hi_done"), sem("k_ready")
        q_mm, q_hi_done, q_ready = sem("q_mm"), sem("q_hi_done"), sem("q_ready")
        vT_mm, vT_done = sem("vT_mm"), sem("vT_done")
        v_mm, v_hi_done, v_ready = sem("v_mm"), sem("v_hi_done"), sem("v_ready")
        s_mm, term_out, summed = sem("s_mm"), sem("term_out"), sem("summed")
        max_done, shifted = sem("max_done"), sem("shifted")
        exp_done, sum_done, inv_done = sem("exp_done"), sem("sum_done"), sem("inv_done")
        probs_ready = sem("probs_ready")
        pT_mm, pT_hi_done, pT_ready = sem("pT_mm"), sem("pT_hi_done"), sem("pT_ready")
        o_mm, o_hi_done, o_ready = sem("o_mm"), sem("o_hi_done"), sem("o_ready")
        y_mm, y_left = sem("y_mm"), sem("y_left")
        f_mm, f_added = sem("f_mm"), sem("f_added")

        x_groups = x.rearrange("(u n p) d -> u p n d", p=P, n=NT)
        out_groups = out.rearrange("(u n p) d -> u p n d", p=P, n=NT)
        ctx_tiles = ctxT.rearrange("(k p) (u t) -> k u p t", p=P, t=GT)
        wq_heads = wq.rearrange("(k p) (g n) -> g p k n", p=P, n=GQ * HD)
        wk_heads = wkv[:, 0:KVW].rearrange("(k p) (g n) -> g p k n", p=P, n=HD)
        wv_heads = wkv[:, KVW:2 * KVW].rearrange("(k p) (g n) -> g p k n", p=P, n=HD)
        wo_heads = wo.rearrange("(g h p) n -> g p h n", p=P, h=GQ)

        def f32(ap):
            return ap.bitcast(F32)

        def score_term(i, term):
            return S_BANKS[i][:, :, :].rearrange("p i (x two m) -> p (i x) two m", two=2, m=L)[:, :, term, :]

        def acc_group(n):
            return acc[:, n * NT:(n + 1) * NT, :]

        def rest(r):
            u = FFN_ORDER[r - 4]
            return wo_stage[:, :, :] if u < NG else acc_group(u - NG)

        def place(r):
            return r % 2

        block = ctx.enter_context(nc.Block())

        @block.sync
        def _(sp):
            def load_qkv(g, half):
                if not (isinstance(g, int) and half * NKV + g == 0):
                    sp.wait_ge(qkv_ready, half * NKV + g)
                sp.dma_start(wkv_stage[:, 0, :, :], wk_heads[g]).then_inc(kv_loaded, 16)
                sp.dma_start(wkv_stage[:, 1, :, :], wv_heads[g]).then_inc(kv_loaded, 16)
                sp.dma_start(bias_stage[:, :], bqkv[g]).then_inc(kv_loaded, 16)
                sp.dma_start(wq_stage[:, :, :], wq_heads[g]).then_inc(qkv_loaded, 16)

            def load_wo(g, half):
                if not (isinstance(g, int) and half * NKV + g == 0):
                    sp.wait_ge(wo_ready, half * NKV + g)
                sp.dma_start(wo_stage[:, :, :], wo_heads[g]).then_inc(wo_loaded, 16)

            def load_x(r):
                if r:
                    sp.wait_ge(xT_mm, r * NT)
                sp.dma_start(x_stage[:, :, :], x_groups[r]).then_inc(x_loaded, 16)

            def load_ctx(r):
                for k in range(KT):
                    c = r * KT + k
                    if c >= 2:
                        sp.wait_ge(ctx_ready, c - 1)
                    sp.dma_start(ctx_stage[:, c % 2, :], ctx_tiles[k, r]).then_inc(ctx_loaded[c % 2], 16)

            def load_acc(r):
                if r >= NG:
                    sp.wait_ge(y_left, NT + (STEPS - NG + (r - NG) + 1) * NT)
                    sp.dma_start(out_groups[r - NG], acc_group(r - NG)).then_inc(spilled, 16)
                    sp.wait_ge(spilled, 16 * (r - NG + 1))
                sp.dma_start(acc_group(r % NG), x_groups[r]).then_inc(acc_loaded, 16)

            load_x(0)
            load_qkv(0, 0)
            load_ctx(0)
            load_wo(0, 0)
            load_acc(0)
            load_x(1)
            load_ctx(1)
            load_acc(1)
            with sp.Fori(1, NKV) as g:
                load_qkv(g, 0)
                load_wo(g, 0)
            load_x(2)
            load_qkv(0, 1)
            load_ctx(2)
            load_wo(0, 1)
            load_x(3)
            load_acc(2)
            load_ctx(3)
            load_acc(3)
            with sp.Fori(1, NKV) as g:
                load_qkv(g, 1)
                load_wo(g, 1)
            sp.wait_ge(wo_ready, 2 * NKV)
            sp.dma_start(wo_stage[:, :, :], out_groups[FFN_ORDER[0]]).then_inc(rest_loaded, 16)
            sp.dma_start(wq_stage[:, :, :], ffn_wT.rearrange("(k p) o -> p k o", p=P)).then_inc(ffn_loaded, 16)
            sp.dma_start(mask_stage, ffn_maskT.rearrange("(k p) o -> p k o", p=P)).then_inc(ffn_loaded, 16)
            for r in range(4, 8):
                u = FFN_ORDER[r - 4]
                for j in range(NT):
                    sp.wait_ge(f_added, (r - 4) * NT + j + 1)
                    sp.dma_start(out_groups[u, :, j, :], rest(r)[:, j, :]).then_inc(stored, 16)
                if r == 4:
                    sp.wait_ge(stored, 16 * NT)
                    sp.dma_start(wo_stage[:, :, :], out_groups[FFN_ORDER[3]]).then_inc(rest_loaded, 16)
            sp.wait_ge(stored, 16 * 4 * NT)

        @block.gpsimd
        def _(pool):
            pool.dma_start(bo_all[:, :], bo.broadcast_to([P, D])).then_inc(bo_loaded, 16)
            nc.gpsimd.memset(ident[:, :], 0.0).then_inc(ident_zero, 1)
            pool.wait_ge(ident_zero, 1)
            nc.gpsimd.affine_select(out=ident[:, :], in_=ident[:, :], compare_op=ALU.not_equal, fill=1.0,
                                    base=0, pattern=[[-1, P]], channel_multiplier=1).then_inc(ident_ready, 1)

            def kv_parts(G):
                pool.wait_ge(qkv_hi_done, G * 2 + 1)
                nc.gpsimd.tensor_tensor(wkv_lo[:, :, :, :], wkv_stage[:, :, :, :], f32(wkv_hi[:, :, :, :]),
                                        ALU.subtract).then_inc(kv_ready, 1)

            def q_parts(G):
                pool.wait_ge(qkv_hi_done, G * 2 + 2)
                nc.gpsimd.tensor_tensor(wq_lo[:, :, :], wq_stage[:, :, :], f32(wq_hi[:, :, :]),
                                        ALU.subtract).then_inc(qkv_ready, 1)

            def wo_parts(G):
                pool.wait_ge(wo_hi_done, G + 1)
                nc.gpsimd.tensor_tensor(wo_lo[:, :, :], wo_stage[:, :, :], f32(wo_hi[:, :, :]),
                                        ALU.subtract).then_inc(wo_ready, 1)

            def ctx_parts(r, tiles=range(KT)):
                for k in tiles:
                    c = r * KT + k
                    t = slice(place(r) * GT, (place(r) + 1) * GT)
                    pool.wait_ge(ctx_hi_done, c + 1)
                    nc.gpsimd.tensor_tensor(cT_lo[:, k, t], ctx_stage[:, c % 2, :], f32(cT_hi[:, k, t]),
                                            ALU.subtract).then_inc(ctx_ready, 1)

            def acc_parts(r):
                pool.wait_ge(acc_loaded, 16 * (r + 1))
                for t in range((r % NG) * NT, (r % NG) * NT + NT):
                    last = nc.gpsimd.tensor_tensor(acc[:, t, :], acc[:, t, :], bo_all[:, :], ALU.add)
                last.then_inc(acc_ready, 1)

            kv_parts(0)
            ctx_parts(0)
            q_parts(0)
            pool.wait_ge(bo_loaded, 16)
            acc_parts(0)
            ctx_parts(1)
            for half in range(HALVES):
                if half:
                    ctx_parts(2, (0, 1))
                    kv_parts(half * NKV)
                    ctx_parts(2, (2, 3))
                    q_parts(half * NKV)
                    acc_parts(2)
                    ctx_parts(3)
                wo_parts(half * NKV)
                acc_parts(2 * half + 1)
                with pool.Fori(1, NKV) as g:
                    kv_parts(half * NKV + g)
                    q_parts(half * NKV + g)
                    wo_parts(half * NKV + g)
            pool.wait_ge(ffn_hi_done, 1)
            nc.gpsimd.tensor_tensor(wq_lo[:, :, :], wq_stage[:, :, :], f32(wq_hi[:, :, :]),
                                    ALU.subtract).then_inc(ffn_ready, 1)

        @block.scalar
        def _(act):
            def copy(o, i, bias=0.0):
                return nc.scalar.activation(o, i, ACT.Identity, bias=bias)

            def kv_hi_parts(G):
                act.wait_ge(kv_loaded, G * 48 + 48)
                copy(bias_now[:, :], bias_stage[:, :]).then_inc(bias_set, 1)
                copy(wkv_hi[:, :, :, :], wkv_stage[:, :, :, :]).then_inc(qkv_hi_done, 1)

            def wq_hi_part(G):
                act.wait_ge(qkv_loaded, G * 16 + 16)
                copy(wq_hi[:, :, :], wq_stage[:, :, :]).then_inc(qkv_hi_done, 1)

            def wo_hi_part(G):
                act.wait_ge(wo_loaded, G * 16 + 16)
                copy(wo_hi[:, :, :], wo_stage[:, :, :]).then_inc(wo_hi_done, 1)

            def ctx_hi_parts(r, tiles=range(KT)):
                for k in tiles:
                    c = r * KT + k
                    act.wait_ge(ctx_loaded[c % 2], 16 * (c // 2 + 1))
                    copy(cT_hi[:, k, place(r) * GT:(place(r) + 1) * GT], ctx_stage[:, c % 2, :]).then_inc(ctx_hi_done, 1)

            def roots(r):
                act.wait_ge(var_done, r + 1)
                nc.scalar.activation(root[:, :], var[:, :], ACT.Sqrt).then_inc(root_done, 1)

            def xT_hi_parts(r):
                for j in range(NT):
                    act.wait_ge(xT_mm, r * NT + (j + 1))
                    t = place(r) * NT + j
                    copy(xT_hi[:, :, t * P:(t + 1) * P],
                         bank(B_X[j]).rearrange("p (k t) -> p k t", k=KT)).then_inc(xT_hi_done, 1)

            def k_hi_part(S, G, n):
                act.wait_ge(k_mm, S + 1)
                if n == 0:
                    act.wait_ge(bias_set, G + 1)
                copy(k_parts[:, :, 0, :], bank(B_K).rearrange("p (b l) -> p b l", l=L),
                     bias_now[:, GQ:GQ + 1]).then_inc(k_hi_done, 1)

            def q_hi_part(S, h):
                act.wait_ge(q_mm, S * GQ + (h + 1))
                copy(q_hi[:, :, h, :], bank(B_Q[h]).rearrange("p (b l) -> p b l", l=L),
                     bias_now[:, h:h + 1]).then_inc(q_hi_done, 1)

            def vT_part(S):
                act.wait_ge(vT_mm, S + 1)
                copy(vT, bank(B_VT), bias_now[:, GQ + 1:GQ + 2]).then_inc(vT_done, 1)

            def v_hi_part(S):
                act.wait_ge(v_mm, S + 1)
                copy(v_hi[:, :, :], bank(B_V).rearrange("p (t d) -> p t d", d=HD)).then_inc(v_hi_done, 1)

            def score_terms(S):
                for i in range(2):
                    act.wait_ge(s_mm, S * 2 + (i + 1))
                    copy(probs[:, i, :, :], score_term(i, 1)).then_inc(term_out, 1)

            def exps(S):
                for i in range(2):
                    act.wait_ge(shifted, S * 2 + (i + 1))
                    nc.scalar.activation(probs[:, i, :, :], probs[:, i, :, :], ACT.Exp, scale=SCALE).then_inc(exp_done, 1)

            def pT_hi_parts(S):
                for i in range(2):
                    act.wait_ge(pT_mm, S * 2 + (i + 1))
                    copy(pT_hi[:, 2 * i:2 * i + 2, :], ps01[:, i, :].rearrange("p (t q) -> p t q", t=2)).then_inc(pT_hi_done, 1)

            def step(S, G, n, more=True, refill=None):
                if more:
                    k_hi_part(S + 1, G + 1, 1 - n)
                    q_hi_part(S + 1, 0)
                    q_hi_part(S + 1, 1)
                if n == 0:
                    wo_hi_part(G)
                for i in range(4):
                    r, b = i // 2, i % 2
                    act.wait_ge(o_mm, S * 4 + (i + 1))
                    copy(o_hi[:, 2 * r:2 * r + 2, :, b, :].rearrange("p t h l -> p (t h) l"),
                         bank(B_O[i]).rearrange("p (x l) -> p x l", l=L)).then_inc(o_hi_done, 1)
                if refill is not None:
                    if refill < 4:
                        ctx_hi_parts(refill, (0, 1))
                    roots(refill)
                if more:
                    vT_part(S + 1)
                    q_hi_part(S + 1, 2)
                    q_hi_part(S + 1, 3)
                    v_hi_part(S + 1)
                    score_terms(S + 1)
                    exps(S + 1)
                    if n == 0 and (refill is None or refill < 4):
                        kv_hi_parts(G + 1)
                    if refill is not None and refill < 4:
                        ctx_hi_parts(refill, (2, 3))
                    if n == 0 and (refill is None or refill < 4):
                        wq_hi_part(G + 1)
                    pT_hi_parts(S + 1)
                if refill is not None:
                    xT_hi_parts(refill)

            kv_hi_parts(0)
            ctx_hi_parts(0)
            wq_hi_part(0)
            roots(0)
            k_hi_part(0, 0, 0)
            vT_part(0)
            v_hi_part(0)
            xT_hi_parts(0)
            for h in range(GQ):
                q_hi_part(0, h)
            roots(1)
            score_terms(0)
            exps(0)
            ctx_hi_parts(1)
            pT_hi_parts(0)
            xT_hi_parts(1)
            for half in range(HALVES):
                S0, G0 = half * STEPS, half * NKV
                with act.Fori(0, NKV - 1) as g:
                    step(S0 + g * NG, G0 + g, 0)
                    step(S0 + g * NG + 1, G0 + g, 1)
                step(S0 + (STEPS - 2), G0 + (NKV - 1), 0, refill=2 * half + 2)
                if half:
                    act.wait_ge(ffn_masked, 1)
                    copy(wq_hi[:, :, :], wq_stage[:, :, :]).then_inc(ffn_hi_done, 1)
                step(S0 + (STEPS - 1), G0 + (NKV - 1), 1, more=(half == 0), refill=2 * half + 3)
            for r in (6, 7):
                roots(r)
                xT_hi_parts(r)

        @block.vector
        def _(dve):
            def low(o, psum, hi, bias=None):
                if bias is None:
                    return nc.vector.tensor_tensor(o, psum, f32(hi), ALU.subtract)
                return nc.vector.scalar_tensor_tensor(out=o, in0=psum, scalar=bias, in1=f32(hi),
                                                      op0=ALU.add, op1=ALU.subtract)

            def norm_input(r):
                return x_stage[:, :, :] if r < 4 else rest(r)

            def norm_stats(r):
                if r < 4:
                    dve.wait_ge(x_loaded, 16 * (r + 1))
                elif FFN_ORDER[r - 4] < NG:
                    dve.wait_ge(rest_loaded, 16 if r == 4 else 32)
                else:
                    dve.wait_ge(y_left, NT + (2 * STEPS - 2 + FFN_ORDER[r - 4] - NG + 1) * NT)
                for j in range(NT):
                    last = nc.vector.bn_stats(stats[:, j, :], norm_input(r)[:, j, :])
                last.then_inc(stats_done, 1)
                dve.wait_ge(stats_done, r + 1)
                nc.vector.tensor_tensor(mean[:, :], stats[:, :, 1], stats[:, :, 4], ALU.add)
                nc.vector.tensor_tensor(gap[:, :], stats[:, :, 1], stats[:, :, 4], ALU.subtract)
                nc.vector.tensor_tensor(var[:, :], stats[:, :, 2], stats[:, :, 5], ALU.add).then_inc(aggr_done, 1)
                dve.wait_ge(aggr_done, r * 2 + 1)
                nc.vector.tensor_scalar(mean[:, :], mean[:, :], 0.5, None, ALU.mult)
                nc.vector.tensor_tensor(gap[:, :], gap[:, :], gap[:, :], ALU.mult)
                nc.vector.tensor_scalar(var[:, :], var[:, :], 1.0 / D, EPS, ALU.mult, ALU.add).then_inc(aggr_done, 1)
                dve.wait_ge(aggr_done, r * 2 + 2)
                nc.vector.scalar_tensor_tensor(out=var[:, :], in0=gap[:, :], scalar=0.25, in1=var[:, :],
                                               op0=ALU.mult, op1=ALU.add).then_inc(var_done, 1)

            def normed(r):
                dve.wait_ge(root_done, r + 1)
                nc.vector.reciprocal(guess[:, :], root[:, :]).then_inc(newton, 1)
                dve.wait_ge(newton, r * 4 + 1)
                nc.vector.tensor_tensor(square[:, :], guess[:, :], guess[:, :], ALU.mult).then_inc(newton, 1)
                dve.wait_ge(newton, r * 4 + 2)
                nc.vector.tensor_tensor(square[:, :], square[:, :], var[:, :], ALU.mult).then_inc(newton, 1)
                dve.wait_ge(newton, r * 4 + 3)
                nc.vector.tensor_scalar(square[:, :], square[:, :], -0.5, 1.5, ALU.mult, ALU.add).then_inc(newton, 1)
                dve.wait_ge(newton, r * 4 + 4)
                nc.vector.tensor_tensor(rstd[:, :], guess[:, :], square[:, :], ALU.mult).then_inc(rstd_done, 1)
                dve.wait_ge(rstd_done, r + 1)
                for j in range(NT):
                    nc.vector.tensor_scalar(x_stage[:, j, :], norm_input(r)[:, j, :], mean[:, j:j + 1],
                                            rstd[:, j:j + 1], ALU.subtract, ALU.mult).then_inc(xn_done, 1)

            def xT_lo_parts(r):
                for j in range(NT):
                    dve.wait_ge(xT_hi_done, r * NT + (j + 1))
                    t = place(r) * NT + j
                    low(xT_lo[:, :, t * P:(t + 1) * P], bank(B_X[j]).rearrange("p (k t) -> p k t", k=KT),
                        xT_hi[:, :, t * P:(t + 1) * P]).then_inc(xT_ready, 1)

            def k_lo_part(S):
                dve.wait_ge(k_hi_done, S + 1)
                low(k_parts[:, :, 1, :], bank(B_K).rearrange("p (b l) -> p b l", l=L), k_parts[:, :, 0, :],
                    bias_now[:, GQ:GQ + 1]).then_inc(k_ready, 1)

            def q_lo_part(S, h):
                dve.wait_ge(q_hi_done, S * GQ + (h + 1))
                low(q_lo[:, :, h, :], bank(B_Q[h]).rearrange("p (b l) -> p b l", l=L),
                    q_hi[:, :, h, :], bias_now[:, h:h + 1]).then_inc(q_ready, 1)

            def v_lo_part(S):
                dve.wait_ge(v_hi_done, S + 1)
                low(v_lo[:, :, :], bank(B_V).rearrange("p (t d) -> p t d", d=HD), v_hi[:, :, :]).then_inc(v_ready, 1)

            def softmax(S):
                for i in range(2):
                    dve.wait_ge(term_out, S * 2 + (i + 1))
                    nc.vector.tensor_tensor(probs[:, i, :, :], score_term(i, 0), probs[:, i, :, :],
                                            ALU.add).then_inc(summed, 1)
                    dve.wait_ge(summed, S * 2 + (i + 1))
                    nc.vector.tensor_reduce(row_max[:, 8 * i:8 * i + 8], probs[:, i, :, :], AX_X,
                                            ALU.max).then_inc(max_done, 1)
                for i in range(2):
                    dve.wait_ge(max_done, S * 2 + (i + 1))
                    nc.vector.tensor_tensor(probs[:, i, :, :], probs[:, i, :, :],
                                            row_max[:, 8 * i:8 * i + 8].unsqueeze(2).broadcast_to([P, 8, L]),
                                            ALU.subtract).then_inc(shifted, 1)
                for i in range(2):
                    dve.wait_ge(exp_done, S * 2 + (i + 1))
                    last = nc.vector.tensor_reduce(row_sum[:, 8 * i:8 * i + 8], probs[:, i, :, :], AX_X, ALU.add)
                last.then_inc(sum_done, 1)
                dve.wait_ge(sum_done, S + 1)
                nc.vector.reciprocal(row_inv[:, :], row_sum[:, :]).then_inc(inv_done, 1)
                dve.wait_ge(inv_done, S + 1)
                for i in range(2):
                    nc.vector.tensor_tensor(probs[:, i, :, :], probs[:, i, :, :],
                                            row_inv[:, 8 * i:8 * i + 8].unsqueeze(2).broadcast_to([P, 8, L]),
                                            ALU.mult).then_inc(probs_ready, 1)

            def pT_lo_parts(S):
                for i in range(2):
                    dve.wait_ge(pT_hi_done, S * 2 + (i + 1))
                    low(pT_lo[:, 2 * i:2 * i + 2, :], ps01[:, i, :].rearrange("p (t q) -> p t q", t=2),
                        pT_hi[:, 2 * i:2 * i + 2, :]).then_inc(pT_ready, 1)

            def step(S, half, n, more=True, refill=None):
                if more:
                    k_lo_part(S + 1)
                    q_lo_part(S + 1, 0)
                    q_lo_part(S + 1, 1)
                for i in range(4):
                    r, b = i // 2, i % 2
                    dve.wait_ge(o_hi_done, S * 4 + (i + 1))
                    low(o_lo[:, 2 * r:2 * r + 2, :, b, :].rearrange("p t h l -> p (t h) l"),
                        bank(B_O[i]).rearrange("p (x l) -> p x l", l=L),
                        o_hi[:, 2 * r:2 * r + 2, :, b, :].rearrange("p t h l -> p (t h) l")).then_inc(o_ready, 1)
                if refill is not None:
                    norm_stats(refill)
                if more:
                    q_lo_part(S + 1, 2)
                    q_lo_part(S + 1, 3)
                    v_lo_part(S + 1)
                    softmax(S + 1)
                if refill is not None:
                    normed(refill)
                dve.wait_ge(acc_ready, half * NG + n + 1)
                for j in range(NT):
                    t = n * NT + j
                    dve.wait_ge(y_mm, S * NT + (j + 1))
                    nc.vector.tensor_tensor(acc[:, t, :], bank(B_Y[j]), acc[:, t, :], ALU.add).then_inc(y_left, 1)
                if more:
                    pT_lo_parts(S + 1)
                if refill is not None:
                    xT_lo_parts(refill)

            def ffn_sums(r):
                for j in range(NT):
                    dve.wait_ge(f_mm, (r - 4) * NT + (j + 1))
                    nc.vector.tensor_tensor(rest(r)[:, j, :], bank(B_F[j]), rest(r)[:, j, :], ALU.add).then_inc(f_added, 1)

            nc.vector.memset(gap[:, :], 0.0).then_inc(y_left, NT)
            norm_stats(0)
            normed(0)
            k_lo_part(0)
            v_lo_part(0)
            xT_lo_parts(0)
            q_lo_part(0, 0)
            q_lo_part(0, 1)
            q_lo_part(0, 2)
            norm_stats(1)
            q_lo_part(0, 3)
            softmax(0)
            normed(1)
            pT_lo_parts(0)
            xT_lo_parts(1)
            for half in range(HALVES):
                S0 = half * STEPS
                with dve.Fori(0, NKV - 1) as g:
                    step(S0 + g * NG, half, 0)
                    step(S0 + g * NG + 1, half, 1)
                step(S0 + (STEPS - 2), half, 0, refill=2 * half + 2)
                if half:
                    dve.wait_ge(ffn_loaded, 32)
                    nc.vector.tensor_tensor(wq_stage[:, :, :], wq_stage[:, :, :], mask_stage, ALU.mult).then_inc(ffn_masked, 1)
                step(S0 + (STEPS - 1), half, 1, more=(half == 0), refill=2 * half + 3)
            norm_stats(6)
            normed(6)
            ffn_sums(4)
            xT_lo_parts(6)
            ffn_sums(5)
            norm_stats(7)
            normed(7)
            ffn_sums(6)
            xT_lo_parts(7)
            ffn_sums(7)

        @block.tensor
        def _(pe):
            def product(o, pairs):
                for n, ((a_hi, a_lo), (b_hi, b_lo)) in enumerate(pairs):
                    nc.tensor.matmul(o, a_hi, b_hi, start=(n == 0), stop=False)
                    nc.tensor.matmul(o, a_hi, b_lo, start=False, stop=False)
                    mm = nc.tensor.matmul(o, a_lo, b_hi, start=False, stop=(n == len(pairs) - 1))
                return mm

            def turn_x(r):
                for j in range(NT):
                    pe.wait_ge(xn_done, r * NT + (j + 1))
                    for k in range(KT):
                        mm = nc.tensor.transpose(bank(B_X[j])[:, k * P:(k + 1) * P], x_stage[:, j, k * P:(k + 1) * P],
                                                 ident[:, :])
                    mm.then_inc(xT_mm, 1)

            def proj_k(n):
                t = slice(n * GT, (n + 1) * GT)
                product(bank(B_K), [((wkv_hi[:, 0, k, :], wkv_lo[:, 0, k, :]), (cT_hi[:, k, t], cT_lo[:, k, t]))
                                    for k in range(KT)]).then_inc(k_mm, 1)

            def proj_v(n):
                t = slice(n * GT, (n + 1) * GT)
                product(bank(B_VT), [((wkv_hi[:, 1, k, :], wkv_lo[:, 1, k, :]), (cT_hi[:, k, t], cT_lo[:, k, t]))
                                     for k in range(KT)]).then_inc(vT_mm, 1)

            def turn_v(S):
                pe.wait_ge(vT_done, S + 1)
                for j in range(NT):
                    mm = nc.tensor.transpose(bank(B_V)[:, j * P:(j + 1) * P], vT[:, j * P:(j + 1) * P], ident[:, :])
                mm.then_inc(v_mm, 1)

            def proj_q(n, h):
                t = slice(n * GT, (n + 1) * GT)
                product(bank(B_Q[h]), [((wq_hi[:, k, h * HD:(h + 1) * HD], wq_lo[:, k, h * HD:(h + 1) * HD]),
                                        (xT_hi[:, k, t], xT_lo[:, k, t])) for k in range(KT)]).then_inc(q_mm, 1)

            def scores(S):
                for i in range(2):
                    for c in range(8):
                        b, hp = 4 * i + 2 * (c // 4) + c % 2, (c // 2) % 2
                        o = S_BANKS[i][:, c // 4, (c % 4) * 2 * L:(c % 4 + 1) * 2 * L]
                        heads = slice(2 * hp, 2 * hp + 2)
                        nc.tensor.matmul(o, q_hi[:, b, heads, :].rearrange("p h l -> p (h l)"),
                                         k_parts[:, b, :, :].rearrange("p i m -> p (i m)"),
                                         start=True, stop=False, skip_group_check=True)
                        mm = nc.tensor.matmul(o[:, 0:L], q_lo[:, b, heads, :].rearrange("p h l -> p (h l)"),
                                              k_parts[:, b, 0, :], start=False, stop=True, skip_group_check=True)
                    mm.then_inc(s_mm, 1)

            def turn_probs(S):
                for i in range(2):
                    pe.wait_ge(probs_ready, S * 2 + (i + 1))
                    for c in range(4):
                        mm = nc.tensor.transpose(ps01[:, i, c * P:(c + 1) * P],
                                                 probs[:, i, 2 * c:2 * c + 2, :].rearrange("p b m -> p (b m)"),
                                                 ident[:, :])
                    mm.then_inc(pT_mm, 1)

            def attend(r):
                for j in (2 * r, 2 * r + 1):
                    for a, w in ((v_hi, pT_hi), (v_hi, pT_lo), (v_lo, pT_hi)):
                        for b in range(2):
                            o = bank(B_O[2 * r + b])[:, (j % 2) * 256:(j % 2) * 256 + 256]
                            mm = nc.tensor.matmul(o, a[b * L:(b + 1) * L, j, :], w[b * L:(b + 1) * L, j, :],
                                                  start=(a is v_hi and w is pT_hi), stop=(a is v_lo))
                            if j % 2 == 1 and a is v_lo:
                                mm.then_inc(o_mm, 1)

            def project_out():
                for j in range(NT):
                    product(bank(B_Y[j]), [((o_hi[:, j, h, :, :].rearrange("p b l -> p (b l)"),
                                             o_lo[:, j, h, :, :].rearrange("p b l -> p (b l)")),
                                            (wo_hi[:, h, :], wo_lo[:, h, :])) for h in range(GQ)]).then_inc(y_mm, 1)

            def step(S, G, half, n, more=True, refill=None):
                if more:
                    m = 1 - n
                    last = n == 1 and refill is not None
                    filled = 2 * half + 1 if m else 2 * half + 2 if last else 2 * half
                    if m == 0:
                        pe.wait_ge(kv_ready, G + 2)
                    pe.wait_ge(ctx_ready, (filled + 1) * KT)
                    pe.wait_ge(y_left, S * NT + 2)
                    proj_k(m)
                    pe.wait_ge(y_left, S * NT + 4)
                    if m == 0:
                        pe.wait_ge(qkv_ready, G + 2)
                    pe.wait_ge(xT_ready, (filled + 1) * NT)
                    proj_q(m, 0)
                    proj_q(m, 1)
                else:
                    pe.wait_ge(xT_ready, refill * NT)
                pe.wait_ge(pT_ready, S * 2 + 2)
                pe.wait_ge(v_ready, S + 1)
                attend(0)
                attend(1)
                if more:
                    proj_v(m)
                    pe.wait_ge(k_ready, S + 2)
                    proj_q(m, 2)
                    pe.wait_ge(q_ready, S * GQ + (GQ + 2))
                    proj_q(m, 3)
                    turn_v(S + 1)
                pe.wait_ge(o_ready, S * 4 + 4)
                if more:
                    pe.wait_ge(q_ready, S * GQ + 2 * GQ)
                    scores(S + 1)
                    pe.wait_ge(v_ready, S + 2)
                if n == 0:
                    pe.wait_ge(wo_ready, G + 1)
                project_out()
                if more:
                    turn_probs(S + 1)
                if refill is not None:
                    pe.wait_ge(y_left, S * NT + 2 * NT)
                    turn_x(refill)

            def ffn(r):
                pe.wait_ge(xT_ready, (r + 1) * NT)
                for j in range(NT):
                    if r > 4:
                        pe.wait_ge(f_added, (r - 5) * NT + j + 1)
                    t = slice((place(r) * NT + j) * P, (place(r) * NT + j + 1) * P)
                    product(bank(B_F[j]), [((xT_hi[:, k, t], xT_lo[:, k, t]), (wq_hi[:, k, :], wq_lo[:, k, :]))
                                           for k in range(KT)]).then_inc(f_mm, 1)

            pe.wait_ge(ident_ready, 1)
            pe.wait_ge(kv_ready, 1)
            pe.wait_ge(ctx_ready, KT)
            proj_k(0)
            proj_v(0)
            turn_v(0)
            pe.wait_ge(v_ready, 1)
            turn_x(0)
            pe.wait_ge(qkv_ready, 1)
            pe.wait_ge(xT_ready, NT)
            proj_q(0, 0)
            proj_q(0, 1)
            pe.wait_ge(k_ready, 1)
            proj_q(0, 2)
            pe.wait_ge(q_ready, 1)
            proj_q(0, 3)
            pe.wait_ge(q_ready, GQ)
            scores(0)
            turn_probs(0)
            turn_x(1)
            for half in range(HALVES):
                S0, G0 = half * STEPS, half * NKV
                with pe.Fori(0, NKV - 1) as g:
                    step(S0 + g * NG, G0 + g, half, 0)
                    step(S0 + g * NG + 1, G0 + g, half, 1)
                step(S0 + (STEPS - 2), G0 + (NKV - 1), half, 0, refill=2 * half + 2)
                step(S0 + (STEPS - 1), G0 + (NKV - 1), half, 1, more=(half == 0), refill=2 * half + 3)
            pe.wait_ge(ffn_ready, 1)
            ffn(4)
            turn_x(6)
            ffn(5)
            ffn(6)
            turn_x(7)
            ffn(7)


def kernel(x, ctx_4096, L0_xattn_Wq, L0_xattn_bq, L0_xattn_Wkv, L0_xattn_bkv, L0_xattn_Wo, L0_xattn_bo,
           L0_ffn_W, L0_ffn_mask):
    import numpy as np
    import concourse.bacc as bacc
    from concourse.bass_utils import run_bass_kernel_spmd

    B, S, D = x.shape
    HD = 128
    heads = np.asarray(L0_xattn_bq).reshape(8, 4, HD)
    kv_bias = np.asarray(L0_xattn_bkv).reshape(2, 8, HD)
    arrays = {
        "x": np.ascontiguousarray(np.asarray(x).reshape(B * S, D)),
        "ctxT": np.ascontiguousarray(np.asarray(ctx_4096).reshape(B * S, D).T),
        "wq": np.ascontiguousarray(L0_xattn_Wq),
        "bqkv": np.ascontiguousarray(np.concatenate([heads, kv_bias[0][:, None], kv_bias[1][:, None]], axis=1)
                                     .transpose(0, 2, 1)),
        "wkv": np.ascontiguousarray(L0_xattn_Wkv),
        "wo": np.ascontiguousarray(L0_xattn_Wo),
        "bo": np.ascontiguousarray(np.asarray(L0_xattn_bo)[None, :]),
        "ffn_wT": np.ascontiguousarray(np.asarray(L0_ffn_W).T),
        "ffn_maskT": np.ascontiguousarray(np.asarray(L0_ffn_mask).T),
    }
    nc = bacc.Bacc("TRN2", target_bir_lowering=False, num_devices=1)
    args = {n: nc.dram_tensor(n, a.shape, mybir.dt.from_np(a.dtype), kind="ExternalInput").ap() for n, a in arrays.items()}
    out = nc.dram_tensor("out", (B * S, D), F32, kind="ExternalOutput").ap()
    xattn_ffn(nc, out=out, **args)
    r = run_bass_kernel_spmd(nc, [arrays], core_ids=[0])
    return r.results[0]["out"].reshape(B, S, D)
```

```python
from contextlib import ExitStack

import concourse.bass as bass
from concourse import mybir

F32 = mybir.dt.float32
F32R = mybir.dt.float32r
U8 = mybir.dt.uint8
ALU = mybir.AluOpType
ACT = mybir.ActivationFunctionType
AX_X = mybir.AxisListType.X

P = 128
EPS = 1e-5


def xattn_ffn(nc, x, ctxT, wq, bqkv, wkv, wo, bo, ffn_wT, ffn_maskT, out):
    TOKENS, D = x.shape
    NKV, HD, NB = bqkv.shape
    GQ = NB - 2
    L = 64
    KT = D // P
    HALVES = 2
    HT = TOKENS // HALVES
    GT = 512
    NG = HT // GT
    NT = GT // P
    HN = HT // P
    STEPS = NKV * NG
    KVW = NKV * HD
    SCALE = float(HD) ** -0.5
    FFN_ORDER = [0, 2, 3, 1]
    STAGED = [0, 1, 2, 3, 4, 7]
    assert HD == P and HALVES == 2 and NG == 2 and NT == 4 and KT == 4 and GQ == 4 and D == GQ * HD

    with ExitStack() as ctx:
        def sb(name, shape, dt=F32):
            return ctx.enter_context(nc.sbuf_tensor(name, shape, dt))

        def sem(name):
            return ctx.enter_context(nc.semaphore(name))

        xT_hi = sb("xT_hi", [P, KT, HT], F32R)
        xT_lo = sb("xT_lo", [P, KT, HT], F32R)
        cT_hi = sb("cT_hi", [P, KT, HT], F32R)
        cT_lo = sb("cT_lo", [P, KT, HT], F32R)
        acc = sb("acc", [P, HN, D])
        wq_hi = sb("wq_hi", [P, KT, GQ * HD], F32R)
        wq_lo = sb("wq_lo", [P, KT, GQ * HD], F32R)
        wkv_hi = sb("wkv_hi", [P, 2, KT, HD], F32R)
        wkv_lo = sb("wkv_lo", [P, 2, KT, HD], F32R)
        wo_hi = sb("wo_hi", [P, GQ, D], F32R)
        wo_lo = sb("wo_lo", [P, GQ, D], F32R)
        wq_stage = sb("wq_stage", [P, KT, GQ * HD])
        wkv_stage = sb("wkv_stage", [P, 2, KT, HD])
        wo_stage = sb("wo_stage", [P, GQ, D])
        ctx_stage = sb("ctx_stage", [P, 2, GT])
        x_stage = sb("x_stage", [P, NT, D])
        mask_stage = ctx_stage[:, :, :].bitcast(U8).rearrange("p i b -> p (i b)")[:, 0:KT * D].rearrange(
            "p (k o) -> p k o", k=KT)
        bias_stage = sb("bias_stage", [P, NB])
        bias_now = sb("bias_now", [P, NB])
        bo_all = sb("bo_all", [P, D])
        ident = sb("ident", [P, P])
        q_hi = sb("q_hi", [P, GT // L, GQ, L], F32R)
        q_lo = sb("q_lo", [P, GT // L, GQ, L], F32R)
        k_parts = sb("k_parts", [P, GT // L, 2, L], F32R)
        v_hi = sb("v_hi", [P, NT, HD], F32R)
        v_lo = sb("v_lo", [P, NT, HD], F32R)
        probs = sb("probs", [P, 2, 8, L])
        vT = probs[:, 1, :, :].rearrange("p x m -> p (x m)")
        pT_hi = sb("pT_hi", [P, NT, 2 * P], F32R)
        pT_lo = sb("pT_lo", [P, NT, 2 * P], F32R)
        o_hi = sb("o_hi", [P, NT, GQ, 2, L], F32R)
        o_lo = sb("o_lo", [P, NT, GQ, 2, L], F32R)
        row_max = sb("row_max", [P, 16])
        row_sum = sb("row_sum", [P, 16])
        row_inv = sb("row_inv", [P, 16])
        stats = sb("stats", [P, NT, 6])
        mean, gap, var, root, guess, square, rstd = [
            sb(n, [P, NT]) for n in ("mean", "gap", "var", "root", "guess", "square", "rstd")]

        ps01 = ctx.enter_context(nc.psum_tensor("ps01", [P, 2, 512], F32))
        ps = [ctx.enter_context(nc.psum_tensor(f"ps{b}", [P, 512], F32)) for b in range(2, 6)]
        ps67 = ctx.enter_context(nc.psum_tensor("ps67", [P, 2, 512], F32))

        def bank(b):
            return ps01[:, b, :] if b < 2 else ps67[:, b - 6, :] if b >= 6 else ps[b - 2][:, :]

        B_K, B_Q, B_O, B_VT, B_V = 2, [3, 4, 5, 2], [6, 7, 0, 1], 3, 4
        S_BANKS, B_Y, B_T, B_X = [ps67, ps01], [5, 2, 3, 4], [6, 0], [7, 1, 5, 4]
        B_END = [6, 0, 2, 3]

        qkv_loaded, qkv_hi_done, qkv_ready = sem("qkv_loaded"), sem("qkv_hi_done"), sem("qkv_ready")
        wo_loaded, wo_hi_done, wo_ready = sem("wo_loaded"), sem("wo_hi_done"), sem("wo_ready")
        kv_loaded, bias_set = sem("kv_loaded"), sem("bias_set")
        kv_ready = sem("kv_ready")
        wk0_loaded, wk0_hi_done, wk0_ready = sem("wk0_loaded"), sem("wk0_hi_done"), sem("wk0_ready")
        q01_loaded, q01_hi_done, q01_ready = sem("q01_loaded"), sem("q01_hi_done"), sem("q01_ready")
        x0_loaded = [sem(f"x0_loaded{j}") for j in range(NT)]
        root_set, root_left = sem("root_set"), sem("root_left")
        ffn_loaded, ffn_masked = sem("ffn_loaded"), sem("ffn_masked")
        ffn_hi_done, ffn_ready = sem("ffn_hi_done"), sem("ffn_ready")
        x_loaded, acc_loaded, acc_ready = sem("x_loaded"), sem("acc_loaded"), sem("acc_ready")
        ctx_loaded = [sem(f"ctx_loaded{n}") for n in range(2)]
        ctx0_loaded = [sem(f"ctx0_loaded{k}") for k in range(KT)]
        ctx_hi_done, ctx_ready = sem("ctx_hi_done"), sem("ctx_ready")
        bo_loaded, ident_zero, ident_ready = sem("bo_loaded"), sem("ident_zero"), sem("ident_ready")
        spilled, rest_loaded, stored = sem("spilled"), sem("rest_loaded"), sem("stored")
        stats_done, aggr_done, var_done = sem("stats_done"), sem("aggr_done"), sem("var_done")
        root_done, newton, rstd_done = sem("root_done"), sem("newton"), sem("rstd_done")
        xn_done, xT_mm, xT_hi_done, xT_ready = sem("xn_done"), sem("xT_mm"), sem("xT_hi_done"), sem("xT_ready")
        k_mm, k_hi_done, k_ready = sem("k_mm"), sem("k_hi_done"), sem("k_ready")
        q_mm, q_hi_done, q_ready = sem("q_mm"), sem("q_hi_done"), sem("q_ready")
        vT_mm, vT_done = sem("vT_mm"), sem("vT_done")
        v_mm, v_hi_done, v_ready = sem("v_mm"), sem("v_hi_done"), sem("v_ready")
        s_mm, term_out, summed = sem("s_mm"), sem("term_out"), sem("summed")
        max_done, shifted = sem("max_done"), sem("shifted")
        exp_done, sum_done, inv_done = sem("exp_done"), sem("sum_done"), sem("inv_done")
        probs_ready = sem("probs_ready")
        pT_mm, pT_hi_done, pT_ready = sem("pT_mm"), sem("pT_hi_done"), sem("pT_ready")
        o_mm, o_hi_done, o_ready = sem("o_mm"), sem("o_hi_done"), sem("o_ready")
        y_mm, y_left = sem("y_mm"), sem("y_left")
        f_mm, f_added = sem("f_mm"), sem("f_added")

        x_groups = x.rearrange("(u n p) d -> u p n d", p=P, n=NT)
        out_groups = out.rearrange("(u n p) d -> u p n d", p=P, n=NT)
        ctx_tiles = ctxT.rearrange("(k p) (u t) -> k u p t", p=P, t=GT)
        wq_heads = wq.rearrange("(k p) (g n) -> g p k n", p=P, n=GQ * HD)
        wk_heads = wkv[:, 0:KVW].rearrange("(k p) (g n) -> g p k n", p=P, n=HD)
        wv_heads = wkv[:, KVW:2 * KVW].rearrange("(k p) (g n) -> g p k n", p=P, n=HD)
        wo_heads = wo.rearrange("(g h p) n -> g p h n", p=P, h=GQ)

        def f32(ap):
            return ap.bitcast(F32)

        def score_term(i, term):
            return S_BANKS[i][:, :, :].rearrange("p i (x two m) -> p (i x) two m", two=2, m=L)[:, :, term, :]

        def acc_group(n):
            return acc[:, n * NT:(n + 1) * NT, :]

        def rest(r):
            u = FFN_ORDER[r - 4]
            return wo_stage[:, :, :] if u < NG else acc_group(u - NG)

        def place(r):
            return r % 2

        def ctx_staged(r, k):
            return wo_stage[:, k, :] if r == 0 else ctx_stage[:, k % 2, :]

        LAST_REFILL = 2 * HALVES + 1

        block = ctx.enter_context(nc.Block())

        @block.sync
        def _(sp):
            def load_qkv(g, half):
                sp.wait_ge(qkv_ready, half * NKV + g)
                sp.dma_start(wkv_stage[:, 0, :, :], wk_heads[g]).then_inc(kv_loaded, 16)
                sp.dma_start(wkv_stage[:, 1, :, :], wv_heads[g]).then_inc(kv_loaded, 16)
                sp.dma_start(bias_stage[:, :], bqkv[g]).then_inc(kv_loaded, 16)
                sp.dma_start(wq_stage[:, :, :], wq_heads[g]).then_inc(qkv_loaded, 16)

            def load_first():
                for j in range(NT):
                    sp.dma_start(x_stage[:, j, :], x_groups[0, :, j, :]).then_inc(x0_loaded[j], 16)
                sp.dma_start(wkv_stage[:, 0, :, :], wk_heads[0]).then_inc(wk0_loaded, 16)
                for k in range(KT):
                    sp.dma_start(ctx_staged(0, k), ctx_tiles[k, 0]).then_inc(ctx0_loaded[k], 16)
                sp.dma_start(wq_stage[:, :, 0:2 * HD], wq_heads[0, :, :, 0:2 * HD]).then_inc(q01_loaded, 16)
                sp.dma_start(wq_stage[:, :, 2 * HD:], wq_heads[0, :, :, 2 * HD:]).then_inc(qkv_loaded, 16)
                sp.dma_start(bias_stage[:, :], bqkv[0]).then_inc(kv_loaded, 16)
                sp.dma_start(wkv_stage[:, 1, :, :], wv_heads[0]).then_inc(kv_loaded, 16)

            def load_wo(g, half):
                if not (isinstance(g, int) and half * NKV + g == 0):
                    sp.wait_ge(wo_ready, half * NKV + g)
                sp.dma_start(wo_stage[:, :, :], wo_heads[g]).then_inc(wo_loaded, 16)

            def load_x(r):
                sp.wait_ge(xT_mm, r * NT)
                source = x_groups[r] if r < 4 else out_groups[FFN_ORDER[r - 4]]
                sp.dma_start(x_stage[:, :, :], source).then_inc(x_loaded, 16)

            def load_ctx(r, tiles=range(KT)):
                for k in tiles:
                    c = r * KT + k
                    if c >= KT + 2:
                        sp.wait_ge(ctx_ready, c - 1)
                    sp.dma_start(ctx_staged(r, k), ctx_tiles[k, r]).then_inc(ctx_loaded[k % 2], 16)

            def load_acc(r):
                if r >= NG:
                    sp.wait_ge(y_left, NT + (STEPS - NG + (r - NG) + 1) * NT)
                    sp.dma_start(out_groups[r - NG], acc_group(r - NG)).then_inc(spilled, 16)
                    sp.wait_ge(spilled, 16 * (r - NG + 1))
                sp.dma_start(acc_group(r % NG), x_groups[r]).then_inc(acc_loaded, 16)

            load_first()
            sp.wait_ge(ctx_ready, KT)
            load_ctx(1, (0, 1))
            load_x(1)
            load_ctx(1, (2, 3))
            load_wo(0, 0)
            load_acc(0)
            sp.wait_ge(acc_loaded, 16)
            load_acc(1)
            sp.wait_ge(q01_ready, 1)
            sp.wait_ge(kv_ready, 1)
            with sp.Fori(1, NKV) as g:
                load_qkv(g, 0)
                load_wo(g, 0)
            load_x(2)
            load_qkv(0, 1)
            load_ctx(2)
            load_wo(0, 1)
            load_x(3)
            load_acc(2)
            load_ctx(3)
            load_acc(3)
            load_x(4)
            with sp.Fori(1, NKV) as g:
                load_qkv(g, 1)
                load_wo(g, 1)
            sp.wait_ge(wo_ready, 2 * NKV)
            sp.dma_start(wo_stage[:, :, :], out_groups[FFN_ORDER[0]]).then_inc(rest_loaded, 16)
            sp.dma_start(wq_stage[:, :, :], ffn_wT.rearrange("(k p) o -> p k o", p=P)).then_inc(ffn_loaded, 16)
            sp.dma_start(mask_stage, ffn_maskT.rearrange("(k p) o -> p k o", p=P)).then_inc(ffn_loaded, 16)
            load_x(7)
            for r in range(4, 8):
                u = FFN_ORDER[r - 4]
                for j in range(NT):
                    sp.wait_ge(f_added, (r - 4) * NT + j + 1)
                    sp.dma_start(out_groups[u, :, j, :], rest(r)[:, j, :]).then_inc(stored, 16)
                if r == 4:
                    sp.wait_ge(stored, 16 * NT)
                    sp.dma_start(wo_stage[:, :, :], out_groups[FFN_ORDER[3]]).then_inc(rest_loaded, 16)
            sp.wait_ge(stored, 16 * 4 * NT)

        @block.gpsimd
        def _(pool):
            pool.dma_start(bo_all[:, :], bo.broadcast_to([P, D])).then_inc(bo_loaded, 16)
            nc.gpsimd.memset(ident[:, :], 0.0).then_inc(ident_zero, 1)
            pool.wait_ge(ident_zero, 1)
            nc.gpsimd.affine_select(out=ident[:, :], in_=ident[:, :], compare_op=ALU.not_equal, fill=1.0,
                                    base=0, pattern=[[-1, P]], channel_multiplier=1).then_inc(ident_ready, 1)

            def kv_parts(G):
                pool.wait_ge(qkv_hi_done, G * 2 + 1)
                nc.gpsimd.tensor_tensor(wkv_lo[:, :, :, :], wkv_stage[:, :, :, :], f32(wkv_hi[:, :, :, :]),
                                        ALU.subtract).then_inc(kv_ready, 1)

            def q_parts(G):
                pool.wait_ge(qkv_hi_done, G * 2 + 2)
                nc.gpsimd.tensor_tensor(wq_lo[:, :, :], wq_stage[:, :, :], f32(wq_hi[:, :, :]),
                                        ALU.subtract).then_inc(qkv_ready, 1)

            def wo_parts(G):
                pool.wait_ge(wo_hi_done, G + 1)
                nc.gpsimd.tensor_tensor(wo_lo[:, :, :], wo_stage[:, :, :], f32(wo_hi[:, :, :]),
                                        ALU.subtract).then_inc(wo_ready, 1)

            def ctx_parts(r, tiles=range(KT)):
                for k in tiles:
                    t = slice(place(r) * GT, (place(r) + 1) * GT)
                    pool.wait_ge(ctx_hi_done, r * KT + k + 1)
                    nc.gpsimd.tensor_tensor(cT_lo[:, k, t], ctx_staged(r, k), f32(cT_hi[:, k, t]),
                                            ALU.subtract).then_inc(ctx_ready, 1)

            def acc_parts(r):
                pool.wait_ge(acc_loaded, 16 * (r + 1))
                for t in range((r % NG) * NT, (r % NG) * NT + NT):
                    last = nc.gpsimd.tensor_tensor(acc[:, t, :], acc[:, t, :], bo_all[:, :], ALU.add)
                last.then_inc(acc_ready, 1)

            pool.wait_ge(wk0_hi_done, 1)
            nc.gpsimd.tensor_tensor(wkv_lo[:, 0, :, :], wkv_stage[:, 0, :, :], f32(wkv_hi[:, 0, :, :]),
                                    ALU.subtract).then_inc(wk0_ready, 1)
            ctx_parts(0, (2, 3))
            pool.wait_ge(qkv_hi_done, 1)
            nc.gpsimd.tensor_tensor(wq_lo[:, :, 2 * HD:], wq_stage[:, :, 2 * HD:], f32(wq_hi[:, :, 2 * HD:]),
                                    ALU.subtract).then_inc(qkv_ready, 1)
            pool.wait_ge(qkv_hi_done, 2)
            nc.gpsimd.tensor_tensor(wkv_lo[:, 1, :, :], wkv_stage[:, 1, :, :], f32(wkv_hi[:, 1, :, :]),
                                    ALU.subtract).then_inc(kv_ready, 1)
            ctx_parts(1)
            pool.wait_ge(bo_loaded, 16)
            acc_parts(0)
            for half in range(HALVES):
                if half:
                    ctx_parts(2, (0, 1))
                    kv_parts(half * NKV)
                    ctx_parts(2, (2, 3))
                    q_parts(half * NKV)
                    acc_parts(2)
                    ctx_parts(3)
                wo_parts(half * NKV)
                acc_parts(2 * half + 1)
                with pool.Fori(1, NKV) as g:
                    kv_parts(half * NKV + g)
                    q_parts(half * NKV + g)
                    wo_parts(half * NKV + g)
            pool.wait_ge(ffn_hi_done, 1)
            nc.gpsimd.tensor_tensor(wq_lo[:, :, :], wq_stage[:, :, :], f32(wq_hi[:, :, :]),
                                    ALU.subtract).then_inc(ffn_ready, 1)

        @block.scalar
        def _(act):
            def copy(o, i, bias=0.0):
                return nc.scalar.activation(o, i, ACT.Identity, bias=bias)

            def kv_hi_parts(G):
                act.wait_ge(kv_loaded, G * 48 + 32)
                copy(bias_now[:, :], bias_stage[:, :]).then_inc(bias_set, 1)
                copy(wkv_hi[:, :, :, :], wkv_stage[:, :, :, :]).then_inc(qkv_hi_done, 1)

            def wq_hi_part(G):
                act.wait_ge(qkv_loaded, G * 16 + 16)
                copy(wq_hi[:, :, :], wq_stage[:, :, :]).then_inc(qkv_hi_done, 1)

            def wo_hi_part(G):
                act.wait_ge(wo_loaded, G * 16 + 16)
                copy(wo_hi[:, :, :], wo_stage[:, :, :]).then_inc(wo_hi_done, 1)

            def ctx_hi_parts(r, tiles=range(KT)):
                for k in tiles:
                    if r:
                        act.wait_ge(ctx_loaded[k % 2], 16 * (2 * (r - 1) + k // 2 + 1))
                    else:
                        act.wait_ge(ctx0_loaded[k], 16)
                    copy(cT_hi[:, k, place(r) * GT:(place(r) + 1) * GT], ctx_staged(r, k)).then_inc(ctx_hi_done, 1)

            def roots(r):
                act.wait_ge(var_done, r + 1)
                nc.scalar.activation(root[:, :], var[:, :], ACT.Sqrt).then_inc(root_done, 1)

            def xT_hi_parts(r):
                for j in range(NT):
                    act.wait_ge(xT_mm, r * NT + (j + 1))
                    t = place(r) * NT + j
                    copy(xT_hi[:, :, t * P:(t + 1) * P],
                         bank(B_X[j]).rearrange("p (k t) -> p k t", k=KT)).then_inc(xT_hi_done, 1)

            def k_hi_part(S, G, n):
                act.wait_ge(k_mm, S + 1)
                if n == 0:
                    act.wait_ge(bias_set, G + 1)
                copy(k_parts[:, :, 0, :], bank(B_K).rearrange("p (b l) -> p b l", l=L),
                     bias_now[:, GQ:GQ + 1]).then_inc(k_hi_done, 1)

            def q_hi_part(S, h):
                act.wait_ge(q_mm, S * GQ + (h + 1))
                copy(q_hi[:, :, h, :], bank(B_Q[h]).rearrange("p (b l) -> p b l", l=L),
                     bias_now[:, h:h + 1]).then_inc(q_hi_done, 1)

            def vT_part(S):
                act.wait_ge(vT_mm, S + 1)
                copy(vT, bank(B_VT), bias_now[:, GQ + 1:GQ + 2]).then_inc(vT_done, 1)

            def v_hi_part(S):
                act.wait_ge(v_mm, S + 1)
                copy(v_hi[:, :, :], bank(B_V).rearrange("p (t d) -> p t d", d=HD)).then_inc(v_hi_done, 1)

            def score_term_out(S, i):
                act.wait_ge(s_mm, S * 2 + (i + 1))
                copy(probs[:, i, :, :], score_term(i, 1)).then_inc(term_out, 1)

            def exps(S, i):
                act.wait_ge(shifted, S * 2 + (i + 1))
                nc.scalar.activation(probs[:, i, :, :], probs[:, i, :, :], ACT.Exp, scale=SCALE).then_inc(exp_done, 1)

            def values_and_exps(S):
                score_term_out(S, 0)
                vT_part(S)
                exps(S, 0)
                v_hi_part(S)
                score_term_out(S, 1)
                exps(S, 1)

            def pT_hi_part(S, i):
                act.wait_ge(pT_mm, S * 2 + (i + 1))
                copy(pT_hi[:, :, i * P:(i + 1) * P], bank(B_T[i]).rearrange("p (t q) -> p t q", q=P)).then_inc(pT_hi_done, 1)

            def step(S, G, n, more=True, refill=None):
                if more:
                    k_hi_part(S + 1, G + 1, 1 - n)
                    q_hi_part(S + 1, 0)
                    q_hi_part(S + 1, 1)
                if n == 0:
                    wo_hi_part(G)
                for i in range(4):
                    r, b = i // 2, i % 2
                    act.wait_ge(o_mm, S * 4 + (i + 1))
                    copy(o_hi[:, 2 * r:2 * r + 2, :, b, :].rearrange("p t h l -> p (t h) l"),
                         bank((B_O if more else B_END)[i]).rearrange("p (x l) -> p x l", l=L)).then_inc(o_hi_done, 1)
                if not more:
                    xT_hi_parts(refill - 1)
                    act.wait_ge(ffn_masked, 1)
                    copy(wq_hi[:, :, :], wq_stage[:, :, :]).then_inc(ffn_hi_done, 1)
                if refill is not None:
                    if refill < 4:
                        ctx_hi_parts(refill, (0, 1))
                    roots(refill)
                if more:
                    q_hi_part(S + 1, 2)
                    q_hi_part(S + 1, 3)
                    values_and_exps(S + 1)
                    if n == 0 and (refill is None or refill < 4):
                        kv_hi_parts(G + 1)
                    if refill is not None and refill < 4:
                        ctx_hi_parts(refill, (2, 3))
                    if n == 0 and (refill is None or refill < 4):
                        wq_hi_part(G + 1)
                    pT_hi_part(S + 1, 0)
                    pT_hi_part(S + 1, 1)
                if refill is not None and refill != LAST_REFILL - 1:
                    xT_hi_parts(refill)

            act.wait_ge(root_set, 1)
            nc.scalar.activation(root[:, :], root[:, :], ACT.Sqrt).then_inc(root_left, 1)
            act.wait_ge(root_left, 1)
            act.wait_ge(wk0_loaded, 16)
            copy(wkv_hi[:, 0, :, :], wkv_stage[:, 0, :, :]).then_inc(wk0_hi_done, 1)
            roots(0)
            ctx_hi_parts(0)
            xT_hi_parts(0)
            act.wait_ge(q01_loaded, 16)
            copy(wq_hi[:, :, 0:2 * HD], wq_stage[:, :, 0:2 * HD]).then_inc(q01_hi_done, 1)
            act.wait_ge(qkv_loaded, 16)
            copy(wq_hi[:, :, 2 * HD:], wq_stage[:, :, 2 * HD:]).then_inc(qkv_hi_done, 1)
            act.wait_ge(kv_loaded, 32)
            copy(bias_now[:, :], bias_stage[:, :]).then_inc(bias_set, 1)
            copy(wkv_hi[:, 1, :, :], wkv_stage[:, 1, :, :]).then_inc(qkv_hi_done, 1)
            k_hi_part(0, 0, 0)
            q_hi_part(0, 0)
            ctx_hi_parts(1, (0, 1))
            q_hi_part(0, 1)
            roots(1)
            q_hi_part(0, 2)
            ctx_hi_parts(1, (2, 3))
            q_hi_part(0, 3)
            score_term_out(0, 0)
            exps(0, 0)
            vT_part(0)
            v_hi_part(0)
            score_term_out(0, 1)
            exps(0, 1)
            xT_hi_parts(1)
            pT_hi_part(0, 0)
            pT_hi_part(0, 1)
            for half in range(HALVES):
                S0, G0 = half * STEPS, half * NKV
                with act.Fori(0, NKV - 1) as g:
                    step(S0 + g * NG, G0 + g, 0)
                    step(S0 + g * NG + 1, G0 + g, 1)
                step(S0 + (STEPS - 2), G0 + (NKV - 1), 0, refill=2 * half + 2)
                step(S0 + (STEPS - 1), G0 + (NKV - 1), 1, more=(half == 0), refill=2 * half + 3)
            for r in (6, 7):
                roots(r)
                xT_hi_parts(r)

        @block.vector
        def _(dve):
            def low(o, psum, hi, bias=None):
                if bias is None:
                    return nc.vector.tensor_tensor(o, psum, f32(hi), ALU.subtract)
                return nc.vector.scalar_tensor_tensor(out=o, in0=psum, scalar=bias, in1=f32(hi),
                                                      op0=ALU.add, op1=ALU.subtract)

            def norm_input(r):
                return x_stage[:, :, :] if r in STAGED else rest(r)

            def norm_stats(r):
                if r in STAGED[1:]:
                    dve.wait_ge(x_loaded, 16 * STAGED.index(r))
                elif r not in STAGED:
                    dve.wait_ge(y_left, NT + (2 * STEPS - 2 + FFN_ORDER[r - 4] - NG + 1) * NT)
                for j in range(NT):
                    if r == 0:
                        dve.wait_ge(x0_loaded[j], 16)
                    last = nc.vector.bn_stats(stats[:, j, :], norm_input(r)[:, j, :])
                last.then_inc(stats_done, 1)
                dve.wait_ge(stats_done, r + 1)
                nc.vector.tensor_tensor(mean[:, :], stats[:, :, 1], stats[:, :, 4], ALU.add)
                nc.vector.tensor_tensor(gap[:, :], stats[:, :, 1], stats[:, :, 4], ALU.subtract)
                nc.vector.tensor_tensor(var[:, :], stats[:, :, 2], stats[:, :, 5], ALU.add).then_inc(aggr_done, 1)
                dve.wait_ge(aggr_done, r * 2 + 1)
                nc.vector.tensor_scalar(mean[:, :], mean[:, :], 0.5, None, ALU.mult)
                nc.vector.tensor_tensor(gap[:, :], gap[:, :], gap[:, :], ALU.mult)
                nc.vector.tensor_scalar(var[:, :], var[:, :], 1.0 / D, EPS, ALU.mult, ALU.add).then_inc(aggr_done, 1)
                dve.wait_ge(aggr_done, r * 2 + 2)
                nc.vector.scalar_tensor_tensor(out=var[:, :], in0=gap[:, :], scalar=0.25, in1=var[:, :],
                                               op0=ALU.mult, op1=ALU.add).then_inc(var_done, 1)

            def normed(r):
                dve.wait_ge(root_done, r + 1)
                nc.vector.reciprocal(guess[:, :], root[:, :]).then_inc(newton, 1)
                dve.wait_ge(newton, r * 4 + 1)
                nc.vector.tensor_tensor(square[:, :], guess[:, :], guess[:, :], ALU.mult).then_inc(newton, 1)
                dve.wait_ge(newton, r * 4 + 2)
                nc.vector.tensor_tensor(square[:, :], square[:, :], var[:, :], ALU.mult).then_inc(newton, 1)
                dve.wait_ge(newton, r * 4 + 3)
                nc.vector.tensor_scalar(square[:, :], square[:, :], -0.5, 1.5, ALU.mult, ALU.add).then_inc(newton, 1)
                dve.wait_ge(newton, r * 4 + 4)
                nc.vector.tensor_tensor(rstd[:, :], guess[:, :], square[:, :], ALU.mult).then_inc(rstd_done, 1)
                dve.wait_ge(rstd_done, r + 1)
                for j in range(NT):
                    nc.vector.tensor_scalar(x_stage[:, j, :], norm_input(r)[:, j, :], mean[:, j:j + 1],
                                            rstd[:, j:j + 1], ALU.subtract, ALU.mult).then_inc(xn_done, 1)

            def xT_lo_parts(r):
                for j in range(NT):
                    dve.wait_ge(xT_hi_done, r * NT + (j + 1))
                    t = place(r) * NT + j
                    low(xT_lo[:, :, t * P:(t + 1) * P], bank(B_X[j]).rearrange("p (k t) -> p k t", k=KT),
                        xT_hi[:, :, t * P:(t + 1) * P]).then_inc(xT_ready, 1)

            def k_lo_part(S):
                dve.wait_ge(k_hi_done, S + 1)
                low(k_parts[:, :, 1, :], bank(B_K).rearrange("p (b l) -> p b l", l=L), k_parts[:, :, 0, :],
                    bias_now[:, GQ:GQ + 1]).then_inc(k_ready, 1)

            def q_lo_part(S, h):
                dve.wait_ge(q_hi_done, S * GQ + (h + 1))
                low(q_lo[:, :, h, :], bank(B_Q[h]).rearrange("p (b l) -> p b l", l=L),
                    q_hi[:, :, h, :], bias_now[:, h:h + 1]).then_inc(q_ready, 1)

            def v_lo_part(S):
                dve.wait_ge(v_hi_done, S + 1)
                low(v_lo[:, :, :], bank(B_V).rearrange("p (t d) -> p t d", d=HD), v_hi[:, :, :]).then_inc(v_ready, 1)

            def shifted_scores(S, i):
                rows = slice(8 * i, 8 * i + 8)
                n = S * 2 + (i + 1)
                dve.wait_ge(term_out, n)
                nc.vector.tensor_tensor(probs[:, i, :, :], score_term(i, 0), probs[:, i, :, :], ALU.add).then_inc(summed, 1)
                dve.wait_ge(summed, n)
                nc.vector.tensor_reduce(row_max[:, rows], probs[:, i, :, :], AX_X, ALU.max).then_inc(max_done, 1)
                dve.wait_ge(max_done, n)
                nc.vector.tensor_tensor(probs[:, i, :, :], probs[:, i, :, :],
                                        row_max[:, rows].unsqueeze(2).broadcast_to([P, 8, L]),
                                        ALU.subtract).then_inc(shifted, 1)

            def divided(S, i):
                rows = slice(8 * i, 8 * i + 8)
                n = S * 2 + (i + 1)
                dve.wait_ge(exp_done, n)
                nc.vector.tensor_reduce(row_sum[:, rows], probs[:, i, :, :], AX_X, ALU.add).then_inc(sum_done, 1)
                dve.wait_ge(sum_done, n)
                nc.vector.reciprocal(row_inv[:, rows], row_sum[:, rows]).then_inc(inv_done, 1)
                dve.wait_ge(inv_done, n)
                nc.vector.tensor_tensor(probs[:, i, :, :], probs[:, i, :, :],
                                        row_inv[:, rows].unsqueeze(2).broadcast_to([P, 8, L]),
                                        ALU.mult).then_inc(probs_ready, 1)

            def pT_lo_part(S, i):
                dve.wait_ge(pT_hi_done, S * 2 + (i + 1))
                low(pT_lo[:, :, i * P:(i + 1) * P], bank(B_T[i]).rearrange("p (t q) -> p t q", q=P),
                    pT_hi[:, :, i * P:(i + 1) * P]).then_inc(pT_ready, 1)

            def step(S, half, n, more=True, refill=None):
                if more:
                    k_lo_part(S + 1)
                    q_lo_part(S + 1, 0)
                    q_lo_part(S + 1, 1)
                for i in range(4):
                    r, b = i // 2, i % 2
                    dve.wait_ge(o_hi_done, S * 4 + (i + 1))
                    low(o_lo[:, 2 * r:2 * r + 2, :, b, :].rearrange("p t h l -> p (t h) l"),
                        bank((B_O if more else B_END)[i]).rearrange("p (x l) -> p x l", l=L),
                        o_hi[:, 2 * r:2 * r + 2, :, b, :].rearrange("p t h l -> p (t h) l")).then_inc(o_ready, 1)
                if not more:
                    xT_lo_parts(refill - 1)
                    dve.wait_ge(ffn_loaded, 32)
                    nc.vector.tensor_tensor(wq_stage[:, :, :], wq_stage[:, :, :], mask_stage, ALU.mult).then_inc(ffn_masked, 1)
                if refill is not None:
                    norm_stats(refill)
                if more:
                    q_lo_part(S + 1, 2)
                    q_lo_part(S + 1, 3)
                    shifted_scores(S + 1, 0)
                if refill is not None:
                    normed(refill)
                if more:
                    divided(S + 1, 0)
                    v_lo_part(S + 1)
                    shifted_scores(S + 1, 1)
                    divided(S + 1, 1)
                dve.wait_ge(acc_ready, half * NG + n + 1)
                for j in range(NT):
                    t = n * NT + j
                    if more and j == NT - 1:
                        pT_lo_part(S + 1, 0)
                        pT_lo_part(S + 1, 1)
                    dve.wait_ge(y_mm, S * NT + (j + 1))
                    nc.vector.tensor_tensor(acc[:, t, :], bank((B_Y if more else B_END)[j]), acc[:, t, :], ALU.add).then_inc(y_left, 1)
                if refill is not None and refill != LAST_REFILL - 1:
                    xT_lo_parts(refill)

            def ffn_sums(r, tiles=range(NT)):
                if FFN_ORDER[r - 4] < NG:
                    dve.wait_ge(rest_loaded, 16 if r == 4 else 32)
                for j in tiles:
                    dve.wait_ge(f_mm, (r - 4) * NT + (j + 1))
                    nc.vector.tensor_tensor(rest(r)[:, j, :], bank(B_END[j]), rest(r)[:, j, :], ALU.add).then_inc(f_added, 1)

            nc.vector.memset(gap[:, :], 0.0).then_inc(y_left, NT)
            nc.vector.memset(root[:, :], 1.0).then_inc(root_set, 1)
            norm_stats(0)
            normed(0)
            for k in (0, 1):
                dve.wait_ge(ctx_hi_done, k + 1)
                nc.vector.tensor_tensor(cT_lo[:, k, 0:GT], ctx_staged(0, k), f32(cT_hi[:, k, 0:GT]),
                                        ALU.subtract).then_inc(ctx_ready, 1)
            xT_lo_parts(0)
            dve.wait_ge(q01_hi_done, 1)
            nc.vector.tensor_tensor(wq_lo[:, :, 0:2 * HD], wq_stage[:, :, 0:2 * HD], f32(wq_hi[:, :, 0:2 * HD]),
                                    ALU.subtract).then_inc(q01_ready, 1)
            k_lo_part(0)
            q_lo_part(0, 0)
            q_lo_part(0, 1)
            norm_stats(1)
            q_lo_part(0, 2)
            q_lo_part(0, 3)
            shifted_scores(0, 0)
            normed(1)
            v_lo_part(0)
            shifted_scores(0, 1)
            divided(0, 0)
            divided(0, 1)
            xT_lo_parts(1)
            pT_lo_part(0, 0)
            pT_lo_part(0, 1)
            for half in range(HALVES):
                S0 = half * STEPS
                with dve.Fori(0, NKV - 1) as g:
                    step(S0 + g * NG, half, 0)
                    step(S0 + g * NG + 1, half, 1)
                step(S0 + (STEPS - 2), half, 0, refill=2 * half + 2)
                step(S0 + (STEPS - 1), half, 1, more=(half == 0), refill=2 * half + 3)
            norm_stats(6)
            normed(6)
            ffn_sums(4)
            xT_lo_parts(6)
            ffn_sums(5, (0, 1))
            norm_stats(7)
            ffn_sums(5, (2, 3))
            normed(7)
            ffn_sums(6, (0, 1))
            xT_lo_parts(7)
            ffn_sums(6, (2, 3))
            ffn_sums(7)

        @block.tensor
        def _(pe):
            def product(o, pairs, between=None):
                last = 3 * len(pairs) - 1
                for n, ((a_hi, a_lo), (b_hi, b_lo)) in enumerate(pairs):
                    for i, (a, b) in enumerate(((a_hi, b_hi), (a_hi, b_lo), (a_lo, b_hi))):
                        mm = nc.tensor.matmul(o, a, b, start=(3 * n + i == 0), stop=(3 * n + i == last),
                                              skip_group_check=between is not None)
                        if between is not None and 3 * n + i < last:
                            between(3 * n + i)
                return mm

            def turn_x(r, last_y=None):
                for j in range(NT):
                    if last_y is not None and j >= 2:
                        pe.wait_ge(y_left, last_y + (1 if j == 2 else NT))
                    pe.wait_ge(xn_done, r * NT + (j + 1))
                    for k in range(KT):
                        mm = nc.tensor.transpose(bank(B_X[j])[:, k * P:(k + 1) * P], x_stage[:, j, k * P:(k + 1) * P],
                                                 ident[:, :])
                    mm.then_inc(xT_mm, 1)

            def proj_k(n):
                t = slice(n * GT, (n + 1) * GT)
                product(bank(B_K), [((wkv_hi[:, 0, k, :], wkv_lo[:, 0, k, :]), (cT_hi[:, k, t], cT_lo[:, k, t]))
                                    for k in range(KT)]).then_inc(k_mm, 1)

            def proj_q(n, h, between=None):
                t = slice(n * GT, (n + 1) * GT)
                product(bank(B_Q[h]), [((wq_hi[:, k, h * HD:(h + 1) * HD], wq_lo[:, k, h * HD:(h + 1) * HD]),
                                        (xT_hi[:, k, t], xT_lo[:, k, t])) for k in range(KT)], between).then_inc(q_mm, 1)

            def proj_v(n, between):
                t = slice(n * GT, (n + 1) * GT)
                product(bank(B_VT), [((wkv_hi[:, 1, k, :], wkv_lo[:, 1, k, :]), (cT_hi[:, k, t], cT_lo[:, k, t]))
                                     for k in range(KT)], between).then_inc(vT_mm, 1)

            def turn_v(S):
                pe.wait_ge(vT_done, S + 1)
                for j in range(NT):
                    mm = nc.tensor.transpose(bank(B_V)[:, j * P:(j + 1) * P], vT[:, j * P:(j + 1) * P], ident[:, :])
                mm.then_inc(v_mm, 1)

            def score(i, m):
                b = m // 2
                o = S_BANKS[i][:, b // 4, (b % 4) * 2 * L:(b % 4 + 1) * 2 * L]
                heads = slice(2 * i, 2 * i + 2)
                if m % 2 == 0:
                    nc.tensor.matmul(o, q_hi[:, b, heads, :].rearrange("p h l -> p (h l)"),
                                     k_parts[:, b, :, :].rearrange("p i m -> p (i m)"),
                                     start=True, stop=False, skip_group_check=True)
                else:
                    mm = nc.tensor.matmul(o[:, 0:L], q_lo[:, b, heads, :].rearrange("p h l -> p (h l)"),
                                          k_parts[:, b, 0, :], start=False, stop=True, skip_group_check=True)
                    if m == 15:
                        mm.then_inc(s_mm, 1)

            def turn_probs(S, i):
                pe.wait_ge(probs_ready, S * 2 + (i + 1))
                for c in range(NT):
                    mm = nc.tensor.transpose(bank(B_T[i])[:, c * P:(c + 1) * P],
                                             probs[:, i, 2 * c:2 * c + 2, :].rearrange("p b m -> p (b m)"),
                                             ident[:, :])
                mm.then_inc(pT_mm, 1)

            def attend(r, banks=B_O):
                for j in (2 * r, 2 * r + 1):
                    for a, w in ((v_hi, pT_hi), (v_hi, pT_lo), (v_lo, pT_hi)):
                        for b in range(2):
                            o = bank(banks[2 * r + b])[:, (j % 2) * 256:(j % 2) * 256 + 256]
                            mm = nc.tensor.matmul(o, a[b * L:(b + 1) * L, j, :], w[b * L:(b + 1) * L, j, :],
                                                  start=(a is v_hi and w is pT_hi), stop=(a is v_lo))
                            if j % 2 == 1 and a is v_lo:
                                mm.then_inc(o_mm, 1)

            def project_out(next_step=None, between=None, banks=B_Y):
                for j in range(NT):
                    if j == NT - 1 and next_step is not None:
                        turn_probs(next_step, 0)
                        turn_probs(next_step, 1)
                        pe.wait_ge(v_ready, next_step + 1)
                    product(bank(banks[j]), [((o_hi[:, j, h, :, :].rearrange("p b l -> p (b l)"),
                                             o_lo[:, j, h, :, :].rearrange("p b l -> p (b l)")),
                                            (wo_hi[:, h, :], wo_lo[:, h, :])) for h in range(GQ)],
                            between if j == 0 else None).then_inc(y_mm, 1)

            def under_q(S):
                def between(n):
                    score(0, n)
                return between

            def under_v(S):
                def between(n):
                    if n < 5:
                        score(0, 11 + n)
                    elif n == 5:
                        pe.wait_ge(q_ready, (S + 1) * GQ)
                    else:
                        score(1, n - 6)
                return between

            def under_y(S):
                def between(n):
                    if n == 2:
                        turn_v(S)
                    score(1, 5 + n)
                return between

            def step(S, G, half, n, more=True, refill=None):
                if more:
                    m = 1 - n
                    last = n == 1 and refill is not None
                    filled = 2 * half + 1 if m else 2 * half + 2 if last else 2 * half
                    if m == 0:
                        pe.wait_ge(kv_ready, G + 2)
                    pe.wait_ge(ctx_ready, (filled + 1) * KT)
                    pe.wait_ge(y_left, S * NT + 2)
                    proj_k(m)
                    pe.wait_ge(y_left, S * NT + 4)
                    if m == 0:
                        pe.wait_ge(qkv_ready, G + 2)
                    pe.wait_ge(xT_ready, (filled + 1) * NT)
                    proj_q(m, 0)
                    proj_q(m, 1)
                pe.wait_ge(pT_ready, S * 2 + 2)
                pe.wait_ge(v_ready, S + 1)
                if not more:
                    pe.wait_ge(y_left, S * NT + 3)
                attend(0, B_O if more else B_END)
                attend(1, B_O if more else B_END)
                if more:
                    proj_q(m, 2)
                    pe.wait_ge(k_ready, S + 2)
                    pe.wait_ge(q_ready, S * GQ + (GQ + 2))
                    pe.wait_ge(o_ready, S * 4 + 2)
                    proj_q(m, 3, under_q(S + 1))
                    pe.wait_ge(o_ready, S * 4 + 4)
                    proj_v(m, under_v(S + 1))
                else:
                    turn_x(refill - 1, S * NT)
                    pe.wait_ge(o_ready, S * 4 + 4)
                if n == 0:
                    pe.wait_ge(wo_ready, G + 1)
                if more:
                    project_out(S + 1, under_y(S + 1))
                else:
                    project_out(banks=B_END)
                if not more:
                    turn_x(refill)
                elif refill is not None and refill != LAST_REFILL - 1:
                    turn_x(refill, S * NT + NT)

            def ffn(r, tiles=range(NT)):
                pe.wait_ge(xT_ready, (r + 1) * NT)
                for j in tiles:
                    if r == 4:
                        pe.wait_ge(y_left, 2 * STEPS * NT + j + 1)
                    else:
                        pe.wait_ge(f_added, (r - 5) * NT + j + 1)
                    t = slice((place(r) * NT + j) * P, (place(r) * NT + j + 1) * P)
                    product(bank(B_END[j]), [((xT_hi[:, k, t], xT_lo[:, k, t]), (wq_hi[:, k, :], wq_lo[:, k, :]))
                                           for k in range(KT)]).then_inc(f_mm, 1)

            pe.wait_ge(ident_ready, 1)
            turn_x(0)
            pe.wait_ge(wk0_ready, 1)
            pe.wait_ge(ctx_ready, KT)
            proj_k(0)
            pe.wait_ge(q01_ready, 1)
            pe.wait_ge(xT_ready, NT)
            proj_q(0, 0)
            proj_q(0, 1)
            pe.wait_ge(qkv_ready, 1)

            def under_q2(n):
                if n == 5:
                    pe.wait_ge(k_ready, 1)
                    pe.wait_ge(q_ready, 2)
                if n >= 5:
                    score(0, n - 5)

            def under_q3(n):
                if n < 10:
                    score(0, 6 + n)

            def under_first_v(n):
                if n == 5:
                    pe.wait_ge(q_ready, GQ)
                if n >= 5:
                    score(1, n - 5)

            proj_q(0, 2, under_q2)
            proj_q(0, 3, under_q3)
            pe.wait_ge(kv_ready, 1)
            proj_v(0, under_first_v)
            for m in range(6, 16):
                score(1, m)
            turn_v(0)
            pe.wait_ge(summed, 2)
            pe.wait_ge(v_ready, 1)
            turn_x(1)
            turn_probs(0, 0)
            turn_probs(0, 1)
            for half in range(HALVES):
                S0, G0 = half * STEPS, half * NKV
                with pe.Fori(0, NKV - 1) as g:
                    step(S0 + g * NG, G0 + g, half, 0)
                    step(S0 + g * NG + 1, G0 + g, half, 1)
                step(S0 + (STEPS - 2), G0 + (NKV - 1), half, 0, refill=2 * half + 2)
                step(S0 + (STEPS - 1), G0 + (NKV - 1), half, 1, more=(half == 0), refill=2 * half + 3)
            pe.wait_ge(ffn_ready, 1)
            ffn(4)
            turn_x(6)
            ffn(5)
            ffn(6, (0, 1))
            turn_x(7)
            ffn(6, (2, 3))
            ffn(7)


def kernel(x, ctx_4096, L0_xattn_Wq, L0_xattn_bq, L0_xattn_Wkv, L0_xattn_bkv, L0_xattn_Wo, L0_xattn_bo,
           L0_ffn_W, L0_ffn_mask):
    import numpy as np
    import concourse.bacc as bacc
    from concourse.bass_utils import run_bass_kernel_spmd

    B, S, D = x.shape
    HD = 128
    heads = np.asarray(L0_xattn_bq).reshape(8, 4, HD)
    kv_bias = np.asarray(L0_xattn_bkv).reshape(2, 8, HD)
    arrays = {
        "x": np.ascontiguousarray(np.asarray(x).reshape(B * S, D)),
        "ctxT": np.ascontiguousarray(np.asarray(ctx_4096).reshape(B * S, D).T),
        "wq": np.ascontiguousarray(L0_xattn_Wq),
        "bqkv": np.ascontiguousarray(np.concatenate([heads, kv_bias[0][:, None], kv_bias[1][:, None]], axis=1)
                                     .transpose(0, 2, 1)),
        "wkv": np.ascontiguousarray(L0_xattn_Wkv),
        "wo": np.ascontiguousarray(L0_xattn_Wo),
        "bo": np.ascontiguousarray(np.asarray(L0_xattn_bo)[None, :]),
        "ffn_wT": np.ascontiguousarray(np.asarray(L0_ffn_W).T),
        "ffn_maskT": np.ascontiguousarray(np.asarray(L0_ffn_mask).T),
    }
    nc = bacc.Bacc("TRN2", target_bir_lowering=False, num_devices=1)
    args = {n: nc.dram_tensor(n, a.shape, mybir.dt.from_np(a.dtype), kind="ExternalInput").ap() for n, a in arrays.items()}
    out = nc.dram_tensor("out", (B * S, D), F32, kind="ExternalOutput").ap()
    xattn_ffn(nc, out=out, **args)
    r = run_bass_kernel_spmd(nc, [arrays], core_ids=[0])
    return r.results[0]["out"].reshape(B, S, D)
```
